# Optimizing a Trainium2 kernel written in Bass

```python
import numpy as np
import jax
import jax.numpy as jnp

def _softmax(x, axis=-1):
    return jax.nn.softmax(x, axis=axis)

def _gelu(x):
    return jax.nn.gelu(x, approximate=True)

def _silu(x):
    return jax.nn.silu(x)

def _sigmoid(x):
    return jax.nn.sigmoid(x)

def _layernorm(x, axis=-1, eps=1e-05):
    m = jnp.mean(x, axis=axis, keepdims=True)
    v = jnp.var(x, axis=axis, keepdims=True)
    return (x - m) / jnp.sqrt(v + eps)

def _scatter_add(tgt, idx, src, axis=0):
    return tgt.at[idx].add(src)

def _segment_sum(src, seg, n):
    return jax.ops.segment_sum(src, seg, n)
kernel_name = 'mk_gnn_ffn_d1_gnn_r8_111f4b'

def setup_inputs(seed: int=0):
    np.random.seed(seed)
    _w = jnp.asarray

    def _rec_inputs():
        import jax
        import jax.numpy as jnp
        _gk = jax.random.key(seed)
        x = -8.776e-05 + 1 * jax.random.normal(jax.random.fold_in(_gk, 1), (1250, 512), jnp.float32)
        src = jax.random.randint(jax.random.fold_in(_gk, 2), (20000,), 0, 1250, jnp.int32)
        dst = jnp.minimum((1250 * jax.random.uniform(jax.random.fold_in(_gk, 3), (20000,)) ** 2.0).astype(jnp.int32), 9999)
        _o = jnp.argsort(dst, stable=True)
        src = src[_o]
        dst = dst[_o]
        edge_attr_512 = 2.93046e-05 + 1.00006 * jax.random.normal(jax.random.fold_in(_gk, 11), (20000, 512), jnp.float32)
        return (x, src, dst, edge_attr_512)
    x, src, dst, edge_attr_512 = _rec_inputs()

    def _L0_gnn_setup():
        import jax, jax.numpy as jnp
        import numpy as np
        N, E, D = (1250, 20000, 512)
        BN_EPS = 1e-05
        key = jax.random.key(seed)
        k = jax.random.split(key, 6)
        x = jax.random.normal(k[0], (N, D), dtype=jnp.float32)
        edge_index = jax.random.randint(k[1], (2, E), 0, N, dtype=jnp.int32)
        edge_attr = jax.random.normal(k[2], (E, D), dtype=jnp.float32)
        W1 = jax.random.normal(k[3], (D, D), dtype=jnp.float32) * 0.02
        b1 = jnp.zeros((D,), dtype=jnp.float32)
        W2 = jax.random.normal(k[4], (D, D), dtype=jnp.float32) * 0.02
        b2 = jnp.zeros((D,), dtype=jnp.float32)
        gamma = jnp.ones((D,), dtype=jnp.float32)
        beta = jnp.zeros((D,), dtype=jnp.float32)
        return {'x': x, 'edge_index': edge_index, 'edge_attr': edge_attr, 'W1': W1, 'b1': b1, 'W2': W2, 'b2': b2, 'gamma': gamma, 'beta': beta}
    _L0_gnn_all = _L0_gnn_setup()
    _L0_gnn_in = {k: v for k, v in _L0_gnn_all.items() if k in ('W1', 'b1', 'W2', 'b2', 'gamma', 'beta')}
    del _L0_gnn_all

    def _L0_ffn_setup():
        import jax, jax.numpy as jnp
        import numpy as np
        B, S, D, H, E, K = (2, 256, 512, 1024, 8, 2)

        def _moe(x, router_w, w_gate, w_up, w_down):
            bsz, seq, d = x.shape
            flat = x.reshape(-1, d)
            logits = flat @ router_w.T
            topk_vals, topk_idx = jax.lax.top_k(logits, K)
            topk_w = jax.nn.softmax(topk_vals, axis=-1)
            s = flat.shape[0]
            dense_w = jnp.zeros((s, E), dtype=flat.dtype).at[jnp.arange(s)[:, None], topk_idx].add(topk_w)
            g = jnp.einsum('sd,edh->esh', flat, w_gate)
            u = jnp.einsum('sd,edh->esh', flat, w_up)
            y = jnp.einsum('esh,ehd->esd', jax.nn.silu(g) * u, w_down)
            out = jnp.einsum('esd,se->sd', y, dense_w)
            return out.reshape(bsz, seq, d)
        key = jax.random.key(seed)
        k1, k2, k3, k4, k5 = jax.random.split(key, 5)
        return {'x': jax.random.normal(k1, (B, S, D), dtype=jnp.float32), 'router_w': jax.random.normal(k2, (E, D), dtype=jnp.float32) * D ** (-0.5), 'w_gate': jax.random.normal(k3, (E, D, H), dtype=jnp.float32) * D ** (-0.5), 'w_up': jax.random.normal(k4, (E, D, H), dtype=jnp.float32) * D ** (-0.5), 'w_down': jax.random.normal(k5, (E, H, D), dtype=jnp.float32) * H ** (-0.5)}
    _L0_ffn_all = _L0_ffn_setup()
    _L0_ffn_in = {k: v for k, v in _L0_ffn_all.items() if k in ('router_w', 'w_gate', 'w_up', 'w_down')}
    del _L0_ffn_all
    return {'x': x, 'src': src, 'dst': dst, 'edge_attr_512': edge_attr_512, 'L0_gnn_W1': _L0_gnn_in['W1'], 'L0_gnn_b1': _L0_gnn_in['b1'], 'L0_gnn_W2': _L0_gnn_in['W2'], 'L0_gnn_b2': _L0_gnn_in['b2'], 'L0_gnn_gamma': _L0_gnn_in['gamma'], 'L0_gnn_beta': _L0_gnn_in['beta'], 'L0_ffn_router_w': _L0_ffn_in['router_w'], 'L0_ffn_w_gate': _L0_ffn_in['w_gate'], 'L0_ffn_w_up': _L0_ffn_in['w_up'], 'L0_ffn_w_down': _L0_ffn_in['w_down']}

def reference(x, src, dst, edge_attr_512, L0_gnn_W1, L0_gnn_b1, L0_gnn_W2, L0_gnn_b2, L0_gnn_gamma, L0_gnn_beta, L0_ffn_router_w, L0_ffn_w_gate, L0_ffn_w_up, L0_ffn_w_down):
    import jax
    import jax.numpy as jnp

    def _L0_gnn_ref(x, edge_index, edge_attr, W1, b1, W2, b2, gamma, beta):
        import jax, jax.numpy as jnp
        import numpy as np
        N, E, D = (1250, 20000, 512)
        BN_EPS = 1e-05
        src, dst = (edge_index[0], edge_index[1])
        msg = jax.nn.relu(x[src] + edge_attr)
        agg = jax.ops.segment_sum(msg, dst, num_segments=x.shape[0])
        h = x + agg
        h = jax.nn.relu(h @ W1 + b1) @ W2 + b2
        h = x + h
        mean = h.mean(axis=0)
        var = h.var(axis=0)
        h = (h - mean) * jax.lax.rsqrt(var + BN_EPS) * gamma + beta
        return h

    def _L0_ffn_ref(x, router_w, w_gate, w_up, w_down):
        import jax, jax.numpy as jnp
        import numpy as np
        B, S, D, H, E, K = (2, 256, 512, 1024, 8, 2)

        def _moe(x, router_w, w_gate, w_up, w_down):
            bsz, seq, d = x.shape
            flat = x.reshape(-1, d)
            logits = flat @ router_w.T
            topk_vals, topk_idx = jax.lax.top_k(logits, K)
            topk_w = jax.nn.softmax(topk_vals, axis=-1)
            s = flat.shape[0]
            dense_w = jnp.zeros((s, E), dtype=flat.dtype).at[jnp.arange(s)[:, None], topk_idx].add(topk_w)
            g = jnp.einsum('sd,edh->esh', flat, w_gate)
            u = jnp.einsum('sd,edh->esh', flat, w_up)
            y = jnp.einsum('esh,ehd->esd', jax.nn.silu(g) * u, w_down)
            out = jnp.einsum('esd,se->sd', y, dense_w)
            return out.reshape(bsz, seq, d)
        return _moe(x, router_w, w_gate, w_up, w_down)
    edge_index = jnp.stack([src, dst])
    x = x + _L0_gnn_ref(_layernorm(x, axis=-1), edge_index, edge_attr_512, L0_gnn_W1, L0_gnn_b1, L0_gnn_W2, L0_gnn_b2, L0_gnn_gamma, L0_gnn_beta)
    x = x + _L0_ffn_ref(_layernorm(x, axis=-1)[None], L0_ffn_router_w, L0_ffn_w_gate, L0_ffn_w_up, L0_ffn_w_down)[0]
    return x

_drawn_inputs = setup_inputs


def setup_inputs(seed=0):
    import zlib

    import numpy as np

    out = dict(_drawn_inputs(seed))
    spreads = {'L0_gnn_b1': (0.0, 0.497),
     'L0_gnn_b2': (0.0, 0.8),
     'L0_gnn_gamma': (1.0, 0.2),
     'L0_gnn_beta': (0.0, 0.1)}
    factors = {}
    for name, (base, spread) in spreads.items():
        noise = np.random.default_rng([zlib.crc32(name.encode()), seed]).standard_normal(out[name].shape)
        drawn = base * np.exp(spread * noise) if base else spread * noise
        out[name] = jnp.asarray(drawn.astype(out[name].dtype))
    for name, factor in factors.items():
        out[name] = (out[name] * factor).astype(out[name].dtype)
    return out
```

```python
from contextlib import ExitStack

import concourse.bass as bass
from concourse import mybir

F32 = mybir.dt.float32
F16 = mybir.dt.float16
I32 = mybir.dt.int32
ALU = mybir.AluOpType
ACT = mybir.ActivationFunctionType
AX = mybir.AxisListType

P = 128
BANK = 512
EPS = 1e-5
FAR = -3.0e38


def gnn_moe_program(nc, x, src, dst, edge_attr, W1, b1, W2, b2, gamma, beta,
                    router_w, w_gate, w_up, w_down, out):
    N, D = x.shape
    E = src.shape[0]
    NX, _, H = w_gate.shape
    NT = -(-N // P)
    LASTN = N - (NT - 1) * P
    NP = NT * P
    KD, KH = D // P, H // P
    J = 4
    STEP = P * J
    NFULL = E // STEP
    TAILP = (E - NFULL * STEP) // J
    NSTEP = NFULL + 1
    RING = 3
    assert NFULL % RING == 0 and 0 < TAILP < P and TAILP * J == E - NFULL * STEP
    SLOTS = (2 * N + NX * P) // P
    SURE = -(-2 * N // P)
    CHUNKS = [(0, BANK), (BANK, BANK), (2 * BANK, NP - 2 * BANK)]
    NOWHERE = 2048
    GROUPS = [(0, 3), (3, 6), (6, 9), (9, NT)]

    xn_dram = nc.dram_tensor("xn_rows", [N, D], F32, kind="Internal").ap()
    x2_dram = nc.dram_tensor("x2_rows", [NP, D], F32, kind="Internal").ap()
    y_dram = nc.dram_tensor("y_rows", [SLOTS * P, D], F32, kind="Internal").ap()

    with ExitStack() as ctx:
        def sb(name, shape, dt=F32):
            return ctx.enter_context(nc.sbuf_tensor(name, shape, dt))

        def sem(name):
            return ctx.enter_context(nc.semaphore(name))

        RINGW = RING * J * D
        big = sb("big", [P, 2 * RINGW + NT * D])
        ea = big[:, 0:RINGW].rearrange("p (r j d) -> p r j d", r=RING, j=J)
        xg = big[:, RINGW:2 * RINGW].rearrange("p (r j d) -> p r j d", r=RING, j=J)
        agg = big[:, 2 * RINGW:].rearrange("p (c d) -> p c d", c=NT)
        hT = big[:, 0:KD * NP].rearrange("p (k n) -> p k n", k=KD)
        uT = big[:, KD * NP:2 * KD * NP].rearrange("p (k n) -> p k n", k=KD)
        oT = big[:, 2 * RINGW:].rearrange("p (k n) -> p k n", k=KD)
        rows = big[:, 0:SLOTS * D].rearrange("p (s d) -> p s d", s=SLOTS)
        w0 = SLOTS * D
        row_cur = big[:, w0:w0 + D]
        rT = big[:, w0 + D:w0 + 2 * D].rearrange("p (k n) -> p k n", k=KD)
        hid = big[:, w0 + 2 * D:w0 + 2 * D + H]
        hidT = big[:, w0 + 2 * D + H:w0 + 2 * D + 2 * H].rearrange("p (k n) -> p k n", k=KH)
        y_sb = sb("y_sb", [P, D])
        wmem = sb("wmem", [P, 5 * KD * H])
        wg = [wmem[:, q * KD * H:(q + 1) * KD * H].rearrange("p (k h) -> p k h", k=KD) for q in (0, 1)]
        wu = [wmem[:, (2 + q) * KD * H:(3 + q) * KD * H].rearrange("p (k h) -> p k h", k=KD) for q in (0, 1)]
        wd = wmem[:, 4 * KD * H:].rearrange("p (k d) -> p k d", k=KH)
        W1_sb = wmem[:, KD * H:KD * H + KD * D].rearrange("p (k d) -> p k d", k=KD)
        W2_sb = wmem[:, KD * H + KD * D:KD * H + 2 * KD * D].rearrange("p (k d) -> p k d", k=KD)
        o = 3 * KD * H
        ids_i = wmem[0:NSTEP, o:o + 2 * STEP].bitcast(I32).rearrange("g (t e) -> g t e", t=2)
        ids_f = wmem[0:NSTEP, o + 2 * STEP:o + 4 * STEP].rearrange("g (t e) -> g t e", t=2)
        hot = wmem[:, o:o + 2 * NT * P].rearrange("p (t n) -> p t n", n=P)
        slotB = wmem[:, o + 2 * NT * P:o + 2 * NT * (P + SLOTS)].rearrange("p (t s) -> p t s", s=SLOTS)
        yg = wmem[:, 0:2 * NT * D].rearrange("p (t c d) -> p t c d", t=2, c=NT)

        x_sb = sb("x_sb", [P, NT, D])
        xn = sb("xn", [P, NT, D])
        ident = sb("ident", [P, P])
        before = sb("before", [P, P])
        ones = sb("ones", [P, P])
        node_i = wmem[:, 2 * KD * H:2 * KD * H + NP].bitcast(I32)
        node = sb("node", [P, NP], F16)
        onehot = sb("onehot", [P, J, P])
        tok_i = sb("tok_i", [P, NT], I32)
        tok = sb("tok", [P, NT])
        valid = sb("valid", [P, NT])
        mv = sb("mv", [P, NT, 2])
        rstd = sb("rstd", [P, NT])
        stats = sb("stats", [P, NT, 6])
        dstT = sb("dstT", [P, NSTEP, J])
        srcT = sb("srcT", [P, NSTEP, J], I32)
        idx = sb("idx", [P, RING, J], I32)
        span = sb("span", [NSTEP, 2])
        span_t = sb("span_t", [1, 2, NSTEP])
        span_i = sb("span_i", [1, 2, NSTEP], I32)
        span_k = sb("span_k", [1, 2, NSTEP], I32)
        span_f = sb("span_f", [1, 2, NSTEP])
        span_v = sb("span_v", [1, 2, NSTEP], I32)
        vecs = sb("vecs", [4 * KD, P])
        vecT = sb("vecT", [P, 4, KD])
        rw = sb("rw", [NX, D])
        rwT = sb("rwT", [P, KD, NX])
        bst = sb("bst", [P, KD, len(CHUNKS), 6])
        bmv = sb("bmv", [P, KD, 2])
        bsc = sb("bsc", [P, 3, KD])
        em8_i = sb("em8_i", [P, NX], I32)
        em8 = sb("em8", [P, NX])
        L = sb("L", [P, NT, NX])
        L2 = sb("L2", [P, NT, NX])
        t8 = sb("t8", [P, NT, NX])
        t9 = sb("t9", [P, NT, NX])
        M1 = sb("M1", [P, NT, NX])
        M2 = sb("M2", [P, NT, NX])
        M = sb("M", [P, NT, NX])
        Mc = sb("Mc", [P, NT + 1, NX])
        v12 = sb("v12", [P, 2, NT])
        i12 = sb("i12", [P, 2, NT])
        w12 = sb("w12", [P, 2, NT])
        wt = sb("wt", [P, 3, NT])
        cnt_i = sb("cnt_i", [P, 2, NX], I32)
        tiles = sb("tiles", [P, NX])
        first = sb("first", [P, NX])
        tab = sb("tab", [P, 2, NX], I32)
        pos = sb("pos", [P, 2, NT])
        pos_i = sb("pos_i", [P, 2, NT], I32)
        ps_i = sb("ps_i", [P, 2, 2 * NT], I32)
        ps_f = sb("ps_f", [P, 2, 2 * NT])
        slot_i = sb("slot_i", [P, SLOTS], I32)

        ps = ctx.enter_context(nc.psum_tensor("ps", [P, 8, BANK], F32))

        s_const, s_x0, s_ids0 = sem("s_const"), sem("s_x0"), sem("s_ids0")
        s_xin = [sem(f"s_xin{g}") for g in range(len(GROUPS))]
        s_var, s_std, s_xn = sem("s_var"), sem("s_std"), sem("s_xn")
        s_xnd = sem("s_xnd")
        s_aggc = sem("s_aggc")
        s_ids, s_idf, s_span, s_tps = sem("s_ids"), sem("s_idf"), sem("s_span"), sem("s_tps")
        s_idx, s_spanv = sem("s_idx"), sem("s_spanv")
        s_vec, s_w12 = sem("s_vec"), sem("s_w12")
        s_dve = sem("s_dve")
        s_ea = [sem(f"s_ea{r}") for r in range(RING)]
        s_xg = [sem(f"s_xg{r}") for r in range(RING)]
        s_idxc, s_idxr = sem("s_idxc"), sem("s_idxr")
        s_sum, s_msg, s_step = sem("s_sum"), sem("s_msg"), sem("s_step")
        s_hot, s_seg, s_acc = sem("s_hot"), sem("s_seg"), sem("s_acc")
        s_agg = sem("s_agg")
        s_tr, s_trc = sem("s_tr"), [sem("s_trc_even"), sem("s_trc_odd")]
        s_l1, s_l1c, s_l2, s_l2c = sem("s_l1"), sem("s_l1c"), sem("s_l2"), sem("s_l2c")
        s_bvar, s_bstd, s_bsc, s_bn = sem("s_bvar"), sem("s_bstd"), sem("s_bsc"), sem("s_bn")
        s_oTt, s_x1 = sem("s_oTt"), sem("s_x1")
        s_var2, s_std2, s_x2, s_x2d = sem("s_var2"), sem("s_std2"), sem("s_x2"), sem("s_x2d")
        s_x2t, s_x2c, s_log = sem("s_x2t"), sem("s_x2c"), sem("s_log")
        s_d, s_ex, s_M, s_rank = sem("s_d"), sem("s_ex"), sem("s_M"), sem("s_rank")
        s_tab, s_hotr, s_slot, s_sloti = sem("s_tab"), sem("s_hotr"), sem("s_slot"), sem("s_sloti")
        s_rows = sem("s_rows")
        s_wgu = [sem(f"s_wgu{q}") for q in (0, 1)]
        s_wd = sem("s_wd")
        s_rcur, s_rt, s_rT = sem("s_rcur"), sem("s_rt"), sem("s_rT")
        s_gu, s_sig, s_sg, s_hid, s_ht, s_hT = (sem(n) for n in ("s_gu", "s_sig", "s_sg", "s_hid", "s_ht", "s_hT"))
        s_y, s_ysb, s_yst, s_yfree, s_xdone = sem("s_y"), sem("s_ysb"), sem("s_yst"), sem("s_yfree"), sem("s_xdone")
        s_yall, s_yg, s_out, s_outd = sem("s_yall"), sem("s_yg"), sem("s_out"), sem("s_outd")
        s_fin, s_yzero, s_yfill = sem("s_fin"), sem("s_yzero"), sem("s_yfill")

        block = ctx.enter_context(nc.Block())

        def row_tile(n):
            return nc.s_assert_within(n, 0, SLOTS - 1, skip_runtime_bounds_check_because="the tiles of all experts are at most SLOTS")

        def xrows(ap, a, b):
            return ap[a * P:b * P, :].rearrange("(c p) d -> p c d", p=P)

        @block.sync
        def _(sp):
            sp.wait_ge(s_x0, 1)
            for g, (a, b) in enumerate(GROUPS):
                if b < NT:
                    sp.dma_start(x_sb[:, a:b, :], xrows(x, a, b)).then_inc(s_xin[g], 16)
                else:
                    sp.dma_start(x_sb[0:LASTN, NT - 1, :], x[(NT - 1) * P:N, :]).then_inc(s_xin[g], 16)

            def load_edges(g, r, parts):
                e0 = g * STEP
                sp.dma_start(ea[0:parts, r, :, :],
                             edge_attr[bass.ds(e0, parts * J), :].rearrange("(p j) d -> p j d", j=J)
                             ).then_inc(s_ea[r], 16)

            for r in range(RING):
                load_edges(r, r, P)
            with sp.Fori(1, NFULL // RING) as i:
                for r in range(RING):
                    g = i * RING + r
                    sp.wait_ge(s_step, g - RING + 1)
                    load_edges(g, r, P)
            sp.wait_ge(s_step, NFULL - RING + 1)
            load_edges(NFULL, 0, TAILP)

            def load_gu(e, q):
                sp.dma_start(wg[q], w_gate[e].rearrange("(k p) h -> p k h", p=P)).then_inc(s_wgu[q], 16)
                sp.dma_start(wu[q], w_up[e].rearrange("(k p) h -> p k h", p=P)).then_inc(s_wgu[q], 16)

            def load_d(e):
                sp.dma_start(wd, w_down[e].rearrange("(k p) d -> p k d", p=P)).then_inc(s_wd, 16)

            sp.wait_ge(s_spanv, 1)
            load_gu(0, 0)
            load_d(0)
            sp.wait_ge(s_slot, 1)
            load_gu(1, 1)

            def stores(e):
                t, f = (sp.value_load(tab[0:1, k, bass.ds(e, 1)], min_val=1 - k, max_val=SLOTS) for k in (0, 1))
                with sp.Fori(0, t) as j:
                    n = row_tile(f + j)
                    sp.wait_ge(s_ysb, n + 1)
                    sp.dma_start(y_dram[bass.ds(n * P, P), :], y_sb[:, :]).then_inc(s_yst, 16)
                    sp.wait_ge(s_yst, n * 16 + 16)
                    sp.sem_inc(s_yfree, 1)
                sp.wait_ge(s_xdone, e + 1)

            sp.wait_ge(s_yfill, 16 * (SLOTS - SURE))
            sp.wait_ge(s_tab, 1)
            with sp.Fori(0, NX // 2 - 1) as i:
                for q in (0, 1):
                    e = 2 * i + q
                    stores(e)
                    load_d(e + 1)
                    load_gu(e + 2, q)
            stores(NX - 2)
            load_d(NX - 1)
            stores(NX - 1)
            sp.sem_inc(s_yall, 1)
            for c in range(NT):
                sp.wait_ge(s_out, c + 1)
                m = P if c < NT - 1 else LASTN
                sp.dma_start(out[c * P:c * P + m, :], x_sb[0:m, c, :]).then_inc(s_outd, 16)
            sp.wait_ge(s_outd, 16 * NT)

        @block.gpsimd
        def _(pool):
            pool.memset(y_sb[:, :], 0.0).then_inc(s_yzero, 1)
            pool.memset(ident[:, :], 0.0).then_inc(s_fin, 1)
            pool.memset(before[:, :], 1.0).then_inc(s_fin, 1)
            pool.memset(ones[:, :], 1.0).then_inc(s_fin, 1)
            pool.wait_ge(s_fin, 3)
            pool.affine_select(out=ident[:, :], in_=ident[:, :], compare_op=ALU.not_equal, fill=1.0, base=0,
                               pattern=[[-1, P]], channel_multiplier=1).then_inc(s_const, 1)
            pool.affine_select(out=before[:, :], in_=before[:, :], compare_op=ALU.is_gt, fill=0.0, base=0,
                               pattern=[[1, P]], channel_multiplier=-1).then_inc(s_const, 1)
            pool.iota(node_i, pattern=[[1, NP]], base=0, channel_multiplier=0).then_inc(s_const, 1)
            pool.iota(tok_i[:, :], pattern=[[P, NT]], base=0, channel_multiplier=1).then_inc(s_const, 1)
            pool.iota(em8_i[:, :], pattern=[[1, NX]], base=-NX, channel_multiplier=0).then_inc(s_const, 1)

            def gathers(g, count, r, parts):
                pool.tensor_copy(idx[:, r, :], srcT[:, bass.ds(g, 1), :].rearrange("p a j -> p (a j)")
                                 ).then_inc(s_idxc, 1)
                pool.wait_ge(s_idxc, count)
                pool.sem_inc(s_idxr, 1)
                for j in range(J):
                    pool.indirect_dma_start(xg[0:parts, r, j, :], None, xn_dram[:, :],
                                            bass.IndirectOffsetOnAxis(ap=idx[0:parts, r, j:j + 1], axis=0)
                                            ).then_inc(s_xg[r], 16)

            pool.wait_ge(s_idx, 1)
            pool.wait_ge(s_xnd, 16 * len(GROUPS))
            for r in range(RING):
                gathers(r, r + 1, r, P)
            with pool.Fori(1, NFULL // RING) as i:
                for r in range(RING):
                    g = i * RING + r
                    pool.wait_ge(s_sum, g - RING + 1)
                    gathers(g, g + 1, r, P)
            pool.wait_ge(s_sum, NFULL - RING + 1)
            gathers(NFULL, NFULL + 1, 0, TAILP)

            pool.wait_ge(s_sloti, 1)
            pool.wait_ge(s_x2d, 16)
            for s in range(SLOTS):
                pool.indirect_dma_start(rows[:, s, :], None, x2_dram[:, :],
                                        bass.IndirectOffsetOnAxis(ap=slot_i[:, s:s + 1], axis=0)
                                        ).then_inc(s_rows, 16)
            pool.wait_ge(s_yall, 1)
            for c in range(NT):
                for k in (0, 1):
                    pool.indirect_dma_start(yg[:, k, c, :], None, y_dram[:, :],
                                            bass.IndirectOffsetOnAxis(ap=pos_i[:, k, c:c + 1], axis=0)
                                            ).then_inc(s_yg, 16)

        @block.scalar
        def _(act):
            act.wait_ge(s_ids0, 1)
            for t, v in enumerate((src, dst)):
                act.dma_start(ids_i[0:NFULL, t, :], v[0:NFULL * STEP].rearrange("(g e) -> g e", e=STEP)
                              ).then_inc(s_ids, 16)
                act.dma_start(ids_i[NFULL:NSTEP, t, 0:TAILP * J], v[NFULL * STEP:E].rearrange("(g e) -> g e", g=1)
                              ).then_inc(s_ids, 16)
            for t, v in enumerate((b1, b2, gamma, beta)):
                act.dma_start(vecs[t * KD:(t + 1) * KD, :], v.rearrange("(k p) -> k p", p=P)).then_inc(s_vec, 16)
            act.dma_start(rw[:, :], router_w[:, :]).then_inc(s_vec, 16)
            act.dma_start(W1_sb, W1.rearrange("(k p) d -> p k d", p=P)).then_inc(s_w12, 16)
            act.dma_start(W2_sb, W2.rearrange("(k p) d -> p k d", p=P)).then_inc(s_w12, 16)
            act.wait_ge(s_yzero, 1)
            for n in range(SURE, SLOTS):
                act.dma_start(y_dram[n * P:(n + 1) * P, :], y_sb[:, :]).then_inc(s_yfill, 16)
            for g, (a, b) in enumerate(GROUPS):
                act.wait_ge(s_var, g + 1)
                act.activation(rstd[:, a:b], mv[:, a:b, 1], ACT.Sqrt).then_inc(s_std, 1)
                act.wait_ge(s_xn, g + 1)
                if b < NT:
                    act.dma_start(xrows(xn_dram, a, b), xn[:, a:b, :]).then_inc(s_xnd, 16)
                else:
                    act.dma_start(xn_dram[(NT - 1) * P:N, :], xn[0:LASTN, NT - 1, :]).then_inc(s_xnd, 16)
                act.copy(agg[:, a:b, :], xn[:, a:b, :]).then_inc(s_aggc, 1)

            def relu(r, count):
                act.wait_ge(s_sum, count)
                act.activation(ea[:, r, :, :], ea[:, r, :, :], ACT.Relu).then_inc(s_msg, 1)

            with act.Fori(0, NFULL // RING) as i:
                for r in range(RING):
                    relu(r, i * RING + (r + 1))
            relu(0, NSTEP)

            for c in range(0, NT, 2):
                act.wait_ge(s_tr, c + 1)
                act.copy(hT[:, :, c * P:(c + 1) * P],
                         ps[:, 3, :].rearrange("p (k n) -> p k n", k=KD)).then_inc(s_trc[0], 1)
            for n, (lo, w) in enumerate(CHUNKS):
                for m in range(KD):
                    i = n * KD + m
                    act.wait_ge(s_l1, i + 1)
                    act.activation(uT[:, m, lo:lo + w], ps[:, 5 + i % 2, 0:w], ACT.Relu,
                                   bias=vecT[:, 0, m:m + 1]).then_inc(s_l1c, 1)
            act.wait_ge(s_bvar, 1)
            act.activation(bsc[:, 0, :], bmv[:, :, 1], ACT.Sqrt).then_inc(s_bstd, 1)
            act.wait_ge(s_bsc, 1)
            for m in range(KD):
                act.activation(oT[:, m, :], oT[:, m, :], ACT.Identity, bias=bsc[:, 2, m:m + 1],
                               scale=bsc[:, 1, m:m + 1]).then_inc(s_bn, 1)
            act.wait_ge(s_var2, 1)
            act.activation(rstd[:, :], mv[:, :, 1], ACT.Sqrt).then_inc(s_std2, 1)
            act.wait_ge(s_x2, NT)
            act.dma_start(xrows(x2_dram, 0, NT), xn[:, :, :]).then_inc(s_x2d, 16)
            for c in range(NT):
                act.wait_ge(s_x2t, c + 1)
                if c >= 1:
                    act.wait_ge(s_log, c)
                act.copy(hT[:, :, 0:P], ps[:, 3 + c % 2, :].rearrange("p (k n) -> p k n", k=KD)).then_inc(s_x2c, 1)
            act.wait_ge(s_d, 1)
            act.activation(wt[:, 1, :], wt[:, 0, :], ACT.Exp).then_inc(s_ex, 1)

            act.wait_ge(s_tab, 1)
            with act.Fori(0, NX) as e:
                t, f = (act.value_load(tab[0:1, k, bass.ds(e, 1)], min_val=1 - k, max_val=SLOTS) for k in (0, 1))
                with act.Fori(0, t) as j:
                    n = row_tile(f + j)
                    act.wait_ge(s_rt, n + 1)
                    act.copy(rT, ps[:, 7, :].rearrange("p (k n) -> p k n", k=KD)).then_inc(s_rT, 1)
                    act.wait_ge(s_gu, n + 1)
                    act.activation(hid, ps[:, 0:2, :].rearrange("p a b -> p (a b)"), ACT.Silu).then_inc(s_sig, 1)
                    for half in (0, 1):
                        act.wait_ge(s_ht, n * 2 + (half + 1))
                        act.copy(hidT[:, half * 4:half * 4 + 4, :],
                                 ps[:, 4 + half, :].rearrange("p (k n) -> p k n", k=4)).then_inc(s_hT, 1)

        @block.vector
        def _(dve):
            chain = [0]

            def link(ins):
                chain[0] += 1
                ins.then_inc(s_dve, 1)
                dve.wait_ge(s_dve, chain[0])

            def fresh(ins):
                chain[0] += 1
                ins.then_inc(s_dve, 1)

            def settled():
                dve.wait_ge(s_dve, chain[0])

            dve.memset(x_sb[:, NT - 1, :], 0.0).then_inc(s_x0, 1)
            fresh(dve.memset(ids_i[:, 0, :], 0))
            settled()
            dve.memset(ids_i[:, 1, :], NOWHERE).then_inc(s_ids0, 1)
            fresh(dve.memset(Mc[:, 0, :], 0.0))
            fresh(dve.memset(first[:, :], 0.0))
            fresh(dve.memset(ps[:, 0, :], 0.0))
            settled()
            dve.sem_inc(s_acc, 1)
            dve.sem_inc(s_seg, J)
            dve.wait_ge(s_const, 5)
            fresh(dve.tensor_copy(node[:, :], node_i))
            fresh(dve.tensor_copy(tok[:, :], tok_i[:, :]))
            fresh(dve.tensor_copy(em8[:, :], em8_i[:, :]))
            settled()
            link(dve.tensor_scalar(valid[:, :], tok[:, :], float(N), None, ALU.is_lt))
            link(dve.tensor_tensor(tok[:, :], tok[:, :], valid[:, :], ALU.mult))

            dve.wait_ge(s_ids, 64)
            dve.tensor_copy(ids_f, ids_i).then_inc(s_idf, 1)
            dve.wait_ge(s_idf, 1)
            dve.tensor_reduce(span[:, 0:1], ids_f[:, 1, :], AX.X, ALU.min).then_inc(s_span, 1)
            dve.tensor_reduce(span[:, 1:2], ids_f[:, 1, :], AX.X, ALU.max).then_inc(s_span, 1)

            def moments(c):
                fresh(dve.bn_stats(stats[:, c, :], x_sb[:, c, :]))

            for g, (a, b) in enumerate(GROUPS):
                dve.wait_ge(s_xin[g], 16)
                for c in range(a, b):
                    moments(c)
                settled()
                for c in range(a, b):
                    fresh(dve.bn_aggr(mv[:, c, :], stats[:, c, :]))
                settled()
                dve.tensor_scalar(mv[:, a:b, 1], mv[:, a:b, 1], EPS, None, ALU.add).then_inc(s_var, 1)
                dve.wait_ge(s_std, g + 1)
                link(dve.reciprocal(rstd[:, a:b], rstd[:, a:b]))
                for c in range(a, b):
                    ins = dve.tensor_scalar(xn[:, c, :], x_sb[:, c, :], mv[:, c, 0:1], rstd[:, c:c + 1],
                                            ALU.subtract, ALU.mult)
                    if c < b - 1:
                        fresh(ins)
                    else:
                        ins.then_inc(s_xn, 1)
                settled()

            dve.wait_ge(s_tps, 1)
            fresh(dve.tensor_copy(dstT[:, :, :], ps[:, 5, 0:J * NSTEP].rearrange("p (j g) -> p g j", j=J)))
            dve.tensor_copy(srcT[:, :, :], ps[:, 4, 0:J * NSTEP].rearrange("p (j g) -> p g j", j=J)
                            ).then_inc(s_idx, 1)
            dve.wait_ge(s_tps, 2)
            link(dve.tensor_copy(span_i[:, :, :], ps[0:1, 6, 0:2 * NSTEP].rearrange("p (t g) -> p t g", t=2)))
            link(dve.tensor_scalar(span_k[:, :, :], span_i[:, :, :], 7, None, ALU.arith_shift_right))
            link(dve.tensor_copy(span_f[:, :, :], span_k[:, :, :]))
            link(dve.tensor_scalar(span_f[:, :, :], span_f[:, :, :], float(NT - 1), None, ALU.min))
            dve.tensor_copy(span_v[:, :, :], span_f[:, :, :]).then_inc(s_spanv, 1)

            dve.wait_ge(s_vec, 80)
            dve.wait_ge(s_tps, 3)
            fresh(dve.tensor_copy(vecT[:, :, :], ps[:, 7, 0:4 * KD].rearrange("p (t k) -> p t k", t=4)))
            fresh(dve.tensor_copy(rwT[:, :, :], ps[:, 7, 4 * KD:4 * KD + KD * NX].rearrange("p (k e) -> p k e", k=KD)))
            settled()

            def add(r, count):
                dve.wait_ge(s_ea[r], count * 16)
                dve.wait_ge(s_xg[r], count * 16 * J)
                dve.tensor_tensor(ea[:, r, :, :], ea[:, r, :, :], xg[:, r, :, :], ALU.add).then_inc(s_sum, 1)

            unit = dve.alloc_register("unit")
            behind = dve.alloc_register("behind")
            dve.reg_mov(unit, 1)
            dve.reg_mov(behind, 0)

            def accumulate(u):
                k = dve.snap(behind, min_val=0, max_val=NT - 1)
                dve.wait_ge(s_seg, u * J)
                dve.wait_ge(s_acc, u)
                a = agg[:, bass.ds(k, 1), :].rearrange("p a d -> p (a d)")
                b = ps[:, bass.ds((u + 1) % 2, 1), :].rearrange("p a d -> p (a d)")
                dve.tensor_tensor(a, a, b, ALU.add).then_inc(s_acc, 1)

            def segment(g):
                lo, hi = (dve.value_load(span_v[0:1, k, bass.ds(g, 1)], min_val=0, max_val=NT - 1) for k in (0, 1))
                with dve.Fori(lo, hi + 1) as k:
                    u = dve.snap(unit, min_val=1, max_val=NSTEP * NT)
                    for j in range(J):
                        dve.wait_ge(s_seg, u * J - (J - 1) + j)
                        dve.tensor_tensor(onehot[:, j, :], node[:, bass.ds(k * P, P)],
                                          dstT[:, bass.ds(g, 1), j].broadcast_to([P, P]), ALU.is_equal
                                          ).then_inc(s_hot, 1)
                    accumulate(u)
                    dve.reg_mov(behind, k)
                    dve.reg_add(unit, unit, 1)

            dve.wait_ge(s_spanv, 1)
            dve.wait_ge(s_aggc, len(GROUPS))
            add(0, 1)
            with dve.Fori(0, NFULL // RING) as i:
                for r in range(RING):
                    add((r + 1) % RING, i + 1 + (r + 1) // RING)
                    segment(i * RING + r)
            segment(NFULL)
            accumulate(dve.snap(unit, min_val=1, max_val=NSTEP * NT + 1))
            total = dve.snap(unit, min_val=1, max_val=NSTEP * NT + 1)
            dve.wait_ge(s_acc, total + 1)
            dve.sem_inc(s_agg, 1)

            for c in range(1, NT, 2):
                dve.wait_ge(s_tr, c + 1)
                dve.tensor_copy(hT[:, :, c * P:(c + 1) * P],
                                ps[:, 4, :].rearrange("p (k n) -> p k n", k=KD)).then_inc(s_trc[1], 1)
            for n, (lo, w) in enumerate(CHUNKS):
                for m in range(KD):
                    i = n * KD + m
                    dve.wait_ge(s_l2, i + 1)
                    dve.tensor_scalar(oT[:, m, lo:lo + w], ps[:, i % 2, 0:w], vecT[:, 1, m:m + 1], None,
                                      ALU.add).then_inc(s_l2c, 1)
                    dve.wait_ge(s_l2c, i + 1)
                    fresh(dve.bn_stats(bst[:, m, n, :], oT[:, m, lo:min(lo + w, N)]))
            settled()
            for m in range(KD):
                fresh(dve.bn_aggr(bmv[:, m, :], bst[:, m, :, :].rearrange("p n s -> p (n s)")))
            settled()
            dve.tensor_scalar(bmv[:, :, 1], bmv[:, :, 1], EPS, None, ALU.add).then_inc(s_bvar, 1)
            dve.wait_ge(s_bstd, 1)
            link(dve.reciprocal(bsc[:, 0, :], bsc[:, 0, :]))
            link(dve.tensor_tensor(bsc[:, 1, :], bsc[:, 0, :], vecT[:, 2, :], ALU.mult))
            link(dve.tensor_tensor(bsc[:, 0, :], bmv[:, :, 0], bsc[:, 1, :], ALU.mult))
            dve.tensor_tensor(bsc[:, 2, :], vecT[:, 3, :], bsc[:, 0, :], ALU.subtract).then_inc(s_bsc, 1)

            for c in range(NT):
                dve.wait_ge(s_oTt, c + 1)
                dve.tensor_tensor(x_sb[:, c, :], x_sb[:, c, :], ps[:, c % 2, :], ALU.add).then_inc(s_x1, 1)
                dve.wait_ge(s_x1, c + 1)
                moments(c)
            settled()
            for c in range(NT):
                fresh(dve.bn_aggr(mv[:, c, :], stats[:, c, :]))
            settled()
            dve.tensor_scalar(mv[:, :, 1], mv[:, :, 1], EPS, None, ALU.add).then_inc(s_var2, 1)
            dve.wait_ge(s_std2, 1)
            link(dve.reciprocal(rstd[:, :], rstd[:, :]))
            for c in range(NT):
                dve.tensor_scalar(xn[:, c, :], x_sb[:, c, :], mv[:, c, 0:1], rstd[:, c:c + 1],
                                  ALU.subtract, ALU.mult).then_inc(s_x2, 1)

            def spread(v):
                return v.unsqueeze(2).broadcast_to([P, NT, NX])

            em8_b = em8[:, :].unsqueeze(1).broadcast_to([P, NT, NX])
            dve.wait_ge(s_log, NT)
            link(dve.tensor_copy(L[:, :, :], ps[:, 2, 0:NT * NX].rearrange("p (c e) -> p c e", e=NX)))
            for k, (logit, mask) in enumerate(((L, M1), (L2, M2))):
                link(dve.tensor_reduce(v12[:, k, :], logit[:, :, :], AX.X, ALU.max))
                link(dve.tensor_tensor(t8[:, :, :], logit[:, :, :], spread(v12[:, k, :]), ALU.is_equal))
                link(dve.tensor_tensor(t8[:, :, :], t8[:, :, :], em8_b, ALU.mult))
                link(dve.tensor_reduce(i12[:, k, :], t8[:, :, :], AX.X, ALU.min))
                link(dve.tensor_tensor(mask[:, :, :], em8_b, spread(i12[:, k, :]), ALU.is_equal))
                if k == 0:
                    link(dve.scalar_tensor_tensor(out=L2[:, :, :], in0=M1[:, :, :], scalar=FAR, in1=L[:, :, :],
                                                  op0=ALU.mult, op1=ALU.add))
            dve.tensor_tensor(wt[:, 0, :], v12[:, 1, :], v12[:, 0, :], ALU.subtract).then_inc(s_d, 1)
            fresh(dve.tensor_tensor(M1[:, :, :], M1[:, :, :], spread(valid[:, :]), ALU.mult))
            fresh(dve.tensor_tensor(M2[:, :, :], M2[:, :, :], spread(valid[:, :]), ALU.mult))
            settled()
            link(dve.tensor_tensor(M[:, :, :], M1[:, :, :], M2[:, :, :], ALU.add))
            for c in range(NT):
                ins = dve.tensor_tensor(Mc[:, c + 1, :], Mc[:, c, :], M[:, c, :], ALU.add)
                if c < NT - 1:
                    link(ins)
                else:
                    ins.then_inc(s_M, 1)
            dve.wait_ge(s_ex, 1)
            link(dve.tensor_scalar(wt[:, 2, :], wt[:, 1, :], 1.0, None, ALU.add))
            link(dve.reciprocal(w12[:, 0, :], wt[:, 2, :]))
            link(dve.tensor_tensor(w12[:, 1, :], wt[:, 1, :], w12[:, 0, :], ALU.mult))

            dve.wait_ge(s_rank, 1)
            link(dve.tensor_scalar(cnt_i[:, 0, :], ps[:, 1, 0:NX], float(P - 1), None, ALU.add))
            link(dve.tensor_scalar(cnt_i[:, 1, :], cnt_i[:, 0, :], 7, None, ALU.arith_shift_right))
            link(dve.tensor_copy(tiles[:, :], cnt_i[:, 1, :]))
            link(dve.tensor_scalar(tiles[:, :], tiles[:, :], 1.0, None, ALU.max))
            for e in range(1, NX):
                link(dve.tensor_tensor(first[:, e:e + 1], first[:, e - 1:e], tiles[:, e - 1:e], ALU.add))
            fresh(dve.tensor_copy(tab[:, 0, :], tiles[:, :]))
            dve.tensor_copy(tab[:, 1, :], first[:, :]).then_inc(s_tab, 1)
            link(dve.scalar_tensor_tensor(out=t8[:, :, :],
                                          in0=first[:, :].unsqueeze(1).broadcast_to([P, NT, NX]), scalar=float(P),
                                          in1=ps[:, 0, 0:NT * NX].rearrange("p (c e) -> p c e", e=NX),
                                          op0=ALU.mult, op1=ALU.add))
            for k, mask in enumerate((M1, M2)):
                link(dve.tensor_tensor(t9[:, :, :], t8[:, :, :], mask[:, :, :], ALU.mult))
                link(dve.tensor_reduce(pos[:, k, :], t9[:, :, :], AX.X, ALU.add))
            link(dve.tensor_copy(pos_i[:, :, :], pos[:, :, :]))
            flat = pos_i[:, :, :].rearrange("p k c -> p (k c)")
            fresh(dve.tensor_scalar(ps_i[:, 0, :], flat, P - 1, None, ALU.bitwise_and))
            fresh(dve.tensor_scalar(ps_i[:, 1, :], flat, 7, None, ALU.arith_shift_right))
            settled()
            link(dve.tensor_copy(ps_f[:, :, :], ps_i[:, :, :]))
            fresh(dve.tensor_tensor(hot, node[:, 0:P].unsqueeze(1).broadcast_to([P, 2 * NT, P]),
                                    ps_f[:, 0, :].unsqueeze(2).broadcast_to([P, 2 * NT, P]), ALU.is_equal))
            link(dve.tensor_tensor(slotB[:, :, :], node[:, 0:SLOTS].unsqueeze(1).broadcast_to([P, 2 * NT, SLOTS]),
                                   ps_f[:, 1, :].unsqueeze(2).broadcast_to([P, 2 * NT, SLOTS]), ALU.is_equal))
            for k in (0, 1):
                half = slotB[:, k * NT:(k + 1) * NT, :]
                ins = dve.tensor_tensor(half, half, tok[:, :].unsqueeze(2).broadcast_to([P, NT, SLOTS]), ALU.mult)
                fresh(ins)
            settled()
            dve.sem_inc(s_hotr, 1)
            dve.wait_ge(s_slot, 1)
            dve.tensor_copy(slot_i[:, :], ps[:, 2, 0:SLOTS]).then_inc(s_sloti, 1)

            dve.wait_ge(s_yfill, 16 * (SLOTS - SURE))
            dve.sem_inc(s_yfree, 1)
            dve.wait_ge(s_rows, 16 * SLOTS)
            with dve.Fori(0, NX) as e:
                t, f = (dve.value_load(tab[0:1, k, bass.ds(e, 1)], min_val=1 - k, max_val=SLOTS) for k in (0, 1))
                with dve.Fori(0, t) as j:
                    n = row_tile(f + j)
                    dve.tensor_copy(row_cur, rows[:, bass.ds(n, 1), :].rearrange("p a d -> p (a d)")
                                    ).then_inc(s_rcur, 1)
                    dve.wait_ge(s_gu, n + 1)
                    dve.wait_ge(s_sig, n + 1)
                    dve.tensor_tensor(hid, hid, ps[:, 2:4, :].rearrange("p a b -> p (a b)"), ALU.mult
                                      ).then_inc(s_hid, 1)
                    dve.wait_ge(s_y, n + 1)
                    dve.wait_ge(s_yfree, n + 1)
                    dve.tensor_copy(y_sb[:, :], ps[:, 6, :]).then_inc(s_ysb, 1)

            for c in range(NT):
                dve.wait_ge(s_yg, 16 * 2 * NT)
                for k in (0, 1):
                    ins = dve.scalar_tensor_tensor(out=x_sb[:, c, :], in0=yg[:, k, c, :], scalar=w12[:, k, c:c + 1],
                                                   in1=x_sb[:, c, :], op0=ALU.mult, op1=ALU.add)
                    if k == 0:
                        link(ins)
                    else:
                        ins.then_inc(s_out, 1)

        @block.tensor
        def _(pe):
            def turn(bank, c0, source, parts=P, count=None):
                cols = source.shape[-1]
                return pe.transpose(ps[0:cols, bank, c0:c0 + parts], source, ident[0:parts, 0:parts])

            pe.wait_ge(s_const, 2)
            pe.wait_ge(s_idf, 1)
            for t, bank in ((0, 4), (1, 5)):
                for j in range(J):
                    last = turn(bank, j * NSTEP, ids_f[:, t, :].rearrange("g (p j) -> g j p", j=J)[:, j, :], NSTEP)
            last.then_inc(s_tps, 1)
            pe.wait_ge(s_span, 2)
            for t in (0, 1):
                last = turn(6, t * NSTEP, span[:, t:t + 1], NSTEP)
            last.then_inc(s_tps, 1)
            pe.wait_ge(s_vec, 80)
            turn(7, 0, vecs[:, :], 4 * KD)
            for k in range(KD):
                last = turn(7, 4 * KD + k * NX, rw[:, k * P:(k + 1) * P], NX)
            last.then_inc(s_tps, 1)

            unit = pe.alloc_register("unit")
            pe.reg_mov(unit, 1)

            def segment(g, r, count):
                lo, hi = (pe.value_load(span_v[0:1, k, bass.ds(g, 1)], min_val=0, max_val=NT - 1) for k in (0, 1))
                with pe.Fori(lo, hi + 1) as k:
                    u = pe.snap(unit, min_val=1, max_val=NSTEP * NT)
                    pe.wait_ge(s_msg, count)
                    pe.wait_ge(s_acc, u)
                    acc = ps[:, bass.ds(u % 2, 1), :].rearrange("p a d -> p (a d)")
                    for j in range(J):
                        pe.wait_ge(s_hot, u * J - (J - 1) + j)
                        pe.matmul(acc, onehot[:, j, :], ea[:, r, j, :], start=(j == 0), stop=(j == J - 1)
                                  ).then_inc(s_seg, 1)
                    pe.reg_add(unit, unit, 1)
                pe.matmul(ps[:, 2, 0:1], ident[:, :], ident[:, 0:1], start=True, stop=True).then_inc(s_step, 1)

            pe.wait_ge(s_spanv, 1)
            with pe.Fori(0, NFULL // RING) as i:
                for r in range(RING):
                    segment(i * RING + r, r, i * RING + (r + 1))
            segment(NFULL, 0, NSTEP)

            pe.wait_ge(s_agg, 1)
            for c in range(NT):
                if c >= 2:
                    pe.wait_ge(s_trc[c % 2], c // 2)
                for k in range(KD):
                    last = turn(3 + c % 2, k * P, agg[:, c, k * P:(k + 1) * P])
                last.then_inc(s_tr, 1)
            for half in s_trc:
                pe.wait_ge(half, NT // 2)
            pe.wait_ge(s_w12, 32)
            for n, (lo, w) in enumerate(CHUNKS):
                for m in range(KD):
                    i = n * KD + m
                    if i >= 2:
                        pe.wait_ge(s_l1c, i - 1)
                    for k in range(KD):
                        last = pe.matmul(ps[:, 5 + i % 2, 0:w], W1_sb[:, k, m * P:(m + 1) * P], hT[:, k, lo:lo + w],
                                         start=(k == 0), stop=(k == KD - 1))
                    last.then_inc(s_l1, 1)
            for n, (lo, w) in enumerate(CHUNKS):
                pe.wait_ge(s_l1c, (n + 1) * KD)
                for m in range(KD):
                    i = n * KD + m
                    if i >= 2:
                        pe.wait_ge(s_l2c, i - 1)
                    for c in range(lo // P, (lo + w) // P):
                        a = c * P - lo
                        pe.matmul(ps[:, i % 2, a:a + P], xn[:, c, m * P:(m + 1) * P], ident[:, :],
                                  start=(a == 0), stop=False, skip_group_check=True)
                    for k in range(KD):
                        last = pe.matmul(ps[:, i % 2, 0:w], W2_sb[:, k, m * P:(m + 1) * P], uT[:, k, lo:lo + w],
                                         start=False, stop=(k == KD - 1), skip_group_check=True)
                    last.then_inc(s_l2, 1)
            pe.wait_ge(s_bn, KD)
            for c in range(NT):
                if c >= 2:
                    pe.wait_ge(s_x1, c - 1)
                for m in range(KD):
                    last = turn(c % 2, m * P, oT[:, m, c * P:(c + 1) * P])
                last.then_inc(s_oTt, 1)
            for c in range(NT):
                pe.wait_ge(s_x2, c + 1)
                if c >= 2:
                    pe.wait_ge(s_x2c, c - 1)
                for k in range(KD):
                    last = turn(3 + c % 2, k * P, xn[:, c, k * P:(k + 1) * P])
                last.then_inc(s_x2t, 1)
                pe.wait_ge(s_x2c, c + 1)
                for k in range(KD):
                    last = pe.matmul(ps[:, 2, c * NX:(c + 1) * NX], hT[:, k, 0:P], rwT[:, k, :],
                                     start=(k == 0), stop=(k == KD - 1))
                last.then_inc(s_log, 1)
            pe.wait_ge(s_M, 1)
            pe.matmul(ps[:, 0, 0:NT * NX], before[:, :], M[:, :, :].rearrange("p c e -> p (c e)"),
                      start=True, stop=False)
            pe.matmul(ps[:, 0, 0:NT * NX], ones[:, :], Mc[:, 0:NT, :].rearrange("p c e -> p (c e)"),
                      start=False, stop=True)
            pe.matmul(ps[:, 1, 0:NX], ones[:, :], Mc[:, NT, :], start=True, stop=True).then_inc(s_rank, 1)
            pe.wait_ge(s_hotr, 1)
            for t in range(2 * NT):
                last = pe.matmul(ps[:, 2, 0:SLOTS], hot[:, t, :], slotB[:, t, :], start=(t == 0), stop=(t == 2 * NT - 1))
            last.then_inc(s_slot, 1)

            def expert(e, q, round_):
                t, f = (pe.value_load(tab[0:1, k, bass.ds(e, 1)], min_val=1 - k, max_val=SLOTS) for k in (0, 1))
                with pe.Fori(0, t) as j:
                    n = row_tile(f + j)
                    pe.wait_ge(s_wgu[q], round_ * 32)
                    pe.wait_ge(s_rcur, n + 1)
                    for k in range(KD):
                        last = turn(7, k * P, row_cur[:, k * P:(k + 1) * P])
                    last.then_inc(s_rt, 1)
                    pe.wait_ge(s_rT, n + 1)
                    for k in range(KD):
                        for b, w in enumerate((wg[q], wu[q])):
                            for h in range(H // BANK):
                                last = pe.matmul(ps[:, 2 * b + h, :], rT[:, k, :], w[:, k, h * BANK:(h + 1) * BANK],
                                                 start=(k == 0), stop=(k == KD - 1))
                    last.then_inc(s_gu, 1)
                    pe.wait_ge(s_hid, n + 1)
                    for half in (0, 1):
                        for k in range(4):
                            a = (half * 4 + k) * P
                            last = turn(4 + half, k * P, hid[:, a:a + P])
                        last.then_inc(s_ht, 1)
                    pe.wait_ge(s_hT, n * 2 + 2)
                    pe.wait_ge(s_wd, e * 16 + 16)
                    for k in range(KH):
                        last = pe.matmul(ps[:, 6, :], hidT[:, k, :], wd[:, k, :], start=(k == 0), stop=(k == KH - 1))
                    last.then_inc(s_y, 1)
                pe.matmul(ps[:, 7, 0:1], ident[:, :], ident[:, 0:1], start=True, stop=True).then_inc(s_xdone, 1)

            pe.wait_ge(s_tab, 1)
            with pe.Fori(0, NX // 2) as i:
                for q in (0, 1):
                    expert(2 * i + q, q, i + 1)


_INS = ['x', 'src', 'dst', 'edge_attr_512', 'L0_gnn_W1', 'L0_gnn_b1', 'L0_gnn_W2', 'L0_gnn_b2', 'L0_gnn_gamma',
        'L0_gnn_beta', 'L0_ffn_router_w', 'L0_ffn_w_gate', 'L0_ffn_w_up', 'L0_ffn_w_down']


def kernel(**inputs):
    import numpy as _np
    import concourse.bacc as _bacc
    from concourse import mybir as _mybir
    from concourse.bass_utils import run_bass_kernel_spmd as _run

    nc = _bacc.Bacc("TRN2", target_bir_lowering=False, num_devices=1)
    arrays, args = {}, []
    for name in _INS:
        a = _np.ascontiguousarray(inputs[name])
        arrays[f"in_{name}_dram"] = a
        args.append(nc.dram_tensor(f"in_{name}_dram", a.shape, _mybir.dt.from_np(a.dtype), kind="ExternalInput").ap())
    out = nc.dram_tensor("out_0_dram", inputs["x"].shape, _mybir.dt.from_np(_np.dtype("float32")),
                         kind="ExternalOutput").ap()
    gnn_moe_program(nc, *args, out)
    r = _run(nc, [arrays], core_ids=[0])
    return r.results[0]["out_0_dram"]
```

```python
from contextlib import ExitStack

import concourse.bass as bass
from concourse import mybir

F32 = mybir.dt.float32
F32R = mybir.dt.float32r
F16 = mybir.dt.float16
I32 = mybir.dt.int32
ALU = mybir.AluOpType
ACT = mybir.ActivationFunctionType
AX = mybir.AxisListType

P = 128
BANK = 512
EPS = 1e-5
FAR = -3.0e38


def gnn_moe_program(nc, x, src, dst, edge_attr, W1, b1, W2, b2, gamma, beta,
                    router_w, w_gate, w_up, w_down, out):
    N, D = x.shape
    E = src.shape[0]
    NX, _, H = w_gate.shape
    NT = -(-N // P)
    LASTN = N - (NT - 1) * P
    NP = NT * P
    KD, KH = D // P, H // P
    J = 4
    STEP = P * J
    NFULL = E // STEP
    TAILP = (E - NFULL * STEP) // J
    NSTEP = NFULL + 1
    RING = 3
    assert NFULL % RING == 0 and 0 < TAILP < P and TAILP * J == E - NFULL * STEP
    SLOTS = (2 * N + NX * P) // P
    SURE = -(-2 * N // P)
    CHUNKS = [(0, BANK), (BANK, BANK), (2 * BANK, NP - 2 * BANK)]
    NC = len(CHUNKS)
    NOWHERE = 2048
    GROUPS = [(0, 3), (3, 6), (6, 9), (9, NT)]
    HALF = NT // 2
    GUC, DC = KD, 2
    PIECE = 2 * H
    SRING = 3
    RROWS = 8
    assert (GUC + DC) % SRING == 0 and PIECE == KH // DC * D

    xn_dram = nc.dram_tensor("xn_rows", [N, D], F32, kind="Internal").ap()
    x2_dram = nc.dram_tensor("x2_rows", [NP, D], F32, kind="Internal").ap()
    y_dram = nc.dram_tensor("y_rows", [SLOTS * P, D], F32, kind="Internal").ap()

    with ExitStack() as ctx:
        def sb(name, shape, dt=F32):
            return ctx.enter_context(nc.sbuf_tensor(name, shape, dt))

        def sem(name):
            return ctx.enter_context(nc.semaphore(name))

        KB = 1024
        base = -(-nc.sbuf_base // 64) * 64
        O_XN, O_AGG, O_RAW, O_G = 20 * KB, 40 * KB, 60 * KB, 84 * KB
        ctx.enter_context(nc.sbuf_tensor("arena", [P, 188 * KB + 64], mybir.dt.uint8))

        def at(name, offset, shape, dt=F32):
            return nc.alloc_sbuf_tensor_at(name, [P, *shape], dt, offset=base + offset)

        x_sb = at("x_sb", 0, [NT, D])
        xn = at("xn", O_XN, [NT, D])
        rT_h, rT_l = (at(f"rT_{c}", O_XN + i * 2 * KB, [KD, P], F32R) for i, c in enumerate("hl"))
        hid = at("hid", O_XN + 4 * KB, [H])
        hidT_h, hidT_l = (at(f"hidT_{c}", O_XN + (8 + 4 * i) * KB, [KH, P], F32R) for i, c in enumerate("hl"))
        row_cur = at("row_cur", O_XN + 16 * KB, [D])
        agg = at("agg", O_AGG, [NT, D])
        oT = at("oT", O_AGG, [KD, NP])
        rows = at("rows", O_AGG, [RROWS, D])
        raw = at("raw", O_RAW, [SRING, PIECE])
        u32 = raw[:, 2, 0:2 * BANK].rearrange("p (r n) -> p r n", r=2)
        ea = at("ea", O_G, [RING, J, D])
        xg = at("xg", O_G + 24 * KB, [RING, J, D])
        hT_h, hT_l = (at(f"hT_{c}", O_G + i * 20 * KB, [KD, NP], F32R) for i, c in enumerate("hl"))
        uT_h, uT_l = (at(f"uT_{c}", O_G + (40 + 16 * i) * KB, [2, KD, BANK], F32R) for i, c in enumerate("hl"))
        ids_i = nc.alloc_sbuf_tensor_at("ids_i", [NSTEP, 2, STEP], I32, offset=base + O_G + 72 * KB)
        ids_f = nc.alloc_sbuf_tensor_at("ids_f", [NSTEP, 2, STEP], F32, offset=base + O_G + 76 * KB)
        node_i = at("node_i", O_G + 80 * KB, [NP], I32)
        W1_h, W1_l, W2_h, W2_l = (at(n, O_G + (72 + 8 * i) * KB, [KD, D], F32R)
                                  for i, n in enumerate(("W1_h", "W1_l", "W2_h", "W2_l")))
        x2T = at("x2T", O_G + 96 * KB, [2, KD, P])
        hot = at("hot", O_G + 72 * KB, [2 * NT, P], F16)
        slotB = at("slotB", O_G + 77 * KB, [2 * NT, SLOTS], F16)
        gu_h, gu_l = (at(f"gu_{c}", O_G + i * 32 * KB, [GUC, PIECE], F32R) for i, c in enumerate("hl"))
        dn_h, dn_l = (at(f"dn_{c}", O_G + (64 + 16 * i) * KB, [DC, PIECE], F32R) for i, c in enumerate("hl"))
        yg = at("yg", O_G, [2, NT, D])

        y_sb = sb("y_sb", [P, D])
        ident = sb("ident", [P, P])
        before = sb("before", [P, P])
        ones = sb("ones", [P, P])
        node = sb("node", [P, NP], F16)
        onehot = sb("onehot", [P, J, P])
        tok_i = sb("tok_i", [P, NT], I32)
        tok = sb("tok", [P, NT])
        valid = sb("valid", [P, NT])
        mv = sb("mv", [P, NT, 2])
        rstd = sb("rstd", [P, NT])
        shift = sb("shift", [P, NT])
        stats = sb("stats", [P, NT, 6])
        dstT = sb("dstT", [P, NSTEP, J])
        srcT = sb("srcT", [P, NSTEP, J], I32)
        idx = sb("idx", [P, RING, J], I32)
        span = sb("span", [NSTEP, 2])
        span_i = sb("span_i", [1, 2, NSTEP], I32)
        span_f = sb("span_f", [1, 2, NSTEP])
        span_v = sb("span_v", [1, 2, NSTEP], I32)
        vecs = sb("vecs", [4 * KD, P])
        vecT = sb("vecT", [P, 4, KD])
        rw = sb("rw", [NX, D])
        rwT = sb("rwT", [P, KD, NX])
        bst = sb("bst", [P, KD, NC, 6])
        bmv = sb("bmv", [P, KD, 2])
        bsc = sb("bsc", [P, 3, KD])
        em8_i = sb("em8_i", [P, NX], I32)
        em8 = sb("em8", [P, NX])
        L = sb("L", [P, NT, NX])
        L2 = sb("L2", [P, NT, NX])
        t8 = sb("t8", [P, NT, NX])
        t9 = sb("t9", [P, NT, NX])
        M1 = sb("M1", [P, NT, NX])
        M2 = sb("M2", [P, NT, NX])
        M = sb("M", [P, NT, NX])
        v12 = sb("v12", [P, 2, NT])
        i12 = sb("i12", [P, 2, NT])
        w12 = sb("w12", [P, 2, NT])
        wt = sb("wt", [P, 3, NT])
        cnt_i = sb("cnt_i", [P, 2, NX], I32)
        tiles = sb("tiles", [P, NX])
        first = sb("first", [P, NX + 1])
        last_i = sb("last_i", [1, 1], I32)
        cmp7 = sb("cmp7", [1, 2, SLOTS, NX - 1])
        tile_f = sb("tile_f", [1, 2, SLOTS])
        tile_v = sb("tile_v", [1, 2, SLOTS], I32)
        pos = sb("pos", [P, 2, NT])
        pos_i = sb("pos_i", [P, 2, NT], I32)
        ps_i = sb("ps_i", [P, 2, 2 * NT], I32)
        ps_f = sb("ps_f", [P, 2, 2 * NT])
        slot_i = sb("slot_i", [P, SLOTS + 1], I32)
        warm = sb("warm", [1, 2])

        ps = ctx.enter_context(nc.psum_tensor("ps", [P, 8, BANK], F32))

        def sems(names):
            return [sem(n) for n in names.split()]

        s_const, s_padx, s_padids, s_zero, s_fill = sems("s_const s_padx s_padids s_zero s_fill")
        s_xin = [sem(f"s_xin{g}") for g in range(len(GROUPS))]
        s_var, s_std, s_shift, s_xn, s_xnd = sems("s_var s_std s_shift s_xn s_xnd")
        s_ids, s_idf, s_span, s_tps, s_idx, s_spanv = sems("s_ids s_idf s_span s_tps s_idx s_spanv")
        s_vec, s_w12, s_w12h, s_w12l, s_dve = sems("s_vec s_w12 s_w12h s_w12l s_dve")
        s_ea = [sem(f"s_ea{r}") for r in range(RING)]
        s_xg = [sem(f"s_xg{r}") for r in range(RING)]
        s_idxc, s_idxr, s_sum, s_msg, s_step = sems("s_idxc s_idxr s_sum s_msg s_step")
        s_hot, s_seg, s_acc, s_agg = sems("s_hot s_seg s_acc s_agg")
        s_tr, s_trh, s_trl = sems("s_tr s_trh s_trl")
        s_l1, s_u, s_uh, s_ul, s_l2, s_l2c = sems("s_l1 s_u s_uh s_ul s_l2 s_l2c")
        s_bvar, s_bstd, s_bsc, s_bna, s_bnd = sems("s_bvar s_bstd s_bsc s_bna s_bnd")
        s_oTt, s_x1, s_var2, s_std2, s_shift2, s_x2, s_x2d = sems("s_oTt s_x1 s_var2 s_std2 s_shift2 s_x2 s_x2d")
        s_x2t, s_x2ca, s_x2cd, s_log = sems("s_x2t s_x2ca s_x2cd s_log")
        s_d, s_ex, s_M, s_rank = sems("s_d s_ex s_M s_rank")
        s_tab, s_hotr, s_slot, s_sloti = sems("s_tab s_hotr s_slot s_sloti")
        s_rows, s_rrdy, s_rcur, s_rt, s_rh, s_rl = sems("s_rows s_rrdy s_rcur s_rt s_rh s_rl")
        s_raw = [sem(f"s_raw{r}") for r in range(SRING)]
        s_guh, s_gul, s_dnh, s_dnl = sems("s_guh s_gul s_dnh s_dnl")
        s_gu, s_sig, s_hid, s_ht, s_hh, s_hl = sems("s_gu s_sig s_hid s_ht s_hh s_hl")
        s_y, s_ysb, s_yst, s_yall, s_out, s_outd = sems("s_y s_ysb s_yst s_yall s_out s_outd")
        s_yg = [sem(f"s_yg{c}") for c in range(NT)]
        FILLS = 16 * (SLOTS - SURE)

        block = ctx.enter_context(nc.Block())

        def xrows(ap, a, b):
            return ap[a * P:b * P, :].rearrange("(c p) d -> p c d", p=P)

        def row_tile(n):
            return nc.s_assert_within(n, 0, SLOTS, skip_runtime_bounds_check_because="at most SLOTS tiles")

        @block.sync
        def _(sp):
            for g, (a, b) in enumerate(GROUPS):
                if b < NT:
                    sp.dma_start(x_sb[:, a:b, :], xrows(x, a, b)).then_inc(s_xin[g], 16)
                else:
                    sp.wait_ge(s_padx, 1)
                    sp.dma_start(x_sb[0:LASTN, NT - 1, :], x[(NT - 1) * P:N, :]).then_inc(s_xin[g], 16)
            sp.wait_ge(s_ids, 64)

            def load_edges(g, r, parts):
                sp.dma_start(ea[0:parts, r, :, :],
                             edge_attr[bass.ds(g * STEP, parts * J), :].rearrange("(p j) d -> p j d", j=J)
                             ).then_inc(s_ea[r], 16)

            for r in range(RING):
                load_edges(r, r, P)
            with sp.Fori(1, NFULL // RING) as i:
                for r in range(RING):
                    g = i * RING + r
                    sp.wait_ge(s_step, g - RING + 1)
                    load_edges(g, r, P)
            sp.wait_ge(s_step, NFULL - RING + 1)
            load_edges(NFULL, 0, TAILP)

            def load_gu(e, k):
                for half, w in enumerate((w_gate, w_up)):
                    sp.dma_start(raw[:, k % SRING, half * H:(half + 1) * H], w[e, k * P:(k + 1) * P, :]
                                 ).then_inc(s_raw[k % SRING], 16)

            def load_dn(e, c):
                r = (GUC + c) % SRING
                kk = KH // DC
                for half in (0, 1):
                    k0 = c * kk + half * kk // 2
                    sp.dma_start(raw[:, r, half * H:(half + 1) * H].rearrange("p (k d) -> p k d", d=D),
                                 w_down[e, k0 * P:(k0 + kk // 2) * P, :].rearrange("(k p) d -> p k d", p=P)
                                 ).then_inc(s_raw[r], 16)

            sp.wait_ge(s_w12l, 2)
            load_gu(0, 0)
            load_gu(0, 1)
            sp.wait_ge(s_ul, NC * KD)
            load_gu(0, 2)

            def rest(e):
                sp.wait_ge(s_gul, e * GUC + 1)
                load_gu(e, 3)
                for c in range(DC):
                    sp.wait_ge(s_gul, e * GUC + (c + 2))
                    load_dn(e, c)

            rest(0)
            with sp.Fori(1, NX) as e:
                sp.wait_ge(s_gul, e * GUC)
                load_gu(e, 0)
                for k in (1, 2):
                    sp.wait_ge(s_dnl, e * DC - DC + k)
                    load_gu(e, k)
                rest(e)

            for c in range(NT):
                sp.wait_ge(s_out, c + 1)
                m = P if c < NT - 1 else LASTN
                sp.dma_start(out[c * P:c * P + m, :], x_sb[0:m, c, :]).then_inc(s_outd, 16)
            sp.wait_ge(s_outd, 16 * NT)

        @block.gpsimd
        def _(pool):
            pool.memset(ident[:, :], 0.0).then_inc(s_zero, 1)
            pool.memset(before[:, :], 1.0).then_inc(s_zero, 1)
            pool.memset(ones[:, :], 1.0).then_inc(s_zero, 1)
            pool.memset(y_sb[:, :], 0.0).then_inc(s_zero, 1)
            pool.memset(slot_i[:, :], 0).then_inc(s_zero, 1)
            pool.wait_ge(s_zero, 3)
            pool.affine_select(out=ident[:, :], in_=ident[:, :], compare_op=ALU.not_equal, fill=1.0, base=0,
                               pattern=[[-1, P]], channel_multiplier=1).then_inc(s_const, 1)
            pool.affine_select(out=before[:, :], in_=before[:, :], compare_op=ALU.is_gt, fill=0.0, base=0,
                               pattern=[[1, P]], channel_multiplier=-1).then_inc(s_const, 1)
            pool.iota(node_i[:, :], pattern=[[1, NP]], base=0, channel_multiplier=0).then_inc(s_const, 1)
            pool.iota(tok_i[:, :], pattern=[[P, NT]], base=0, channel_multiplier=1).then_inc(s_const, 1)
            pool.iota(em8_i[:, :], pattern=[[1, NX]], base=-NX, channel_multiplier=0).then_inc(s_const, 1)

            def gathers(g, count, r, parts):
                pool.tensor_copy(idx[:, r, :], srcT[:, bass.ds(g, 1), :].rearrange("p a j -> p (a j)")
                                 ).then_inc(s_idxc, 1)
                pool.wait_ge(s_idxc, count)
                pool.sem_inc(s_idxr, 1)
                for j in range(J):
                    pool.indirect_dma_start(xg[0:parts, r, j, :], None, xn_dram[:, :],
                                            bass.IndirectOffsetOnAxis(ap=idx[0:parts, r, j:j + 1], axis=0)
                                            ).then_inc(s_xg[r], 16)

            pool.wait_ge(s_idx, 1)
            pool.wait_ge(s_xnd, 16 * len(GROUPS))
            for r in range(RING):
                gathers(r, r + 1, r, P)
            with pool.Fori(1, NFULL // RING) as i:
                for r in range(RING):
                    g = i * RING + r
                    pool.wait_ge(s_sum, g - RING + 1)
                    gathers(g, g + 1, r, P)
            pool.wait_ge(s_sum, NFULL - RING + 1)
            gathers(NFULL, NFULL + 1, 0, TAILP)

            pool.wait_ge(s_sloti, 1)
            pool.wait_ge(s_x2d, 32)
            for n in range(SLOTS + 1):
                if n >= RROWS:
                    pool.wait_ge(s_rcur, n - RROWS + 1)
                pool.indirect_dma_start(rows[:, n % RROWS, :], None, x2_dram[:, :],
                                        bass.IndirectOffsetOnAxis(ap=slot_i[:, n:n + 1], axis=0)
                                        ).then_inc(s_rows, 16)
                pool.wait_ge(s_rows, 16 * (n + 1))
                pool.sem_inc(s_rrdy, 1)
            pool.wait_ge(s_yall, 1)
            for c in range(NT):
                for k in (0, 1):
                    pool.indirect_dma_start(yg[:, k, c, :], None, y_dram[:, :],
                                            bass.IndirectOffsetOnAxis(ap=pos_i[:, k, c:c + 1], axis=0)
                                            ).then_inc(s_yg[c], 16)

        @block.scalar
        def _(act):
            act.wait_ge(s_padids, 1)
            for t, v in enumerate((src, dst)):
                act.dma_start(ids_i[0:NFULL, t, :], v[0:NFULL * STEP].rearrange("(g e) -> g e", e=STEP)
                              ).then_inc(s_ids, 16)
                act.dma_start(ids_i[NFULL:NSTEP, t, 0:TAILP * J], v[NFULL * STEP:E].rearrange("(g e) -> g e", g=1)
                              ).then_inc(s_ids, 16)
            act.activation(warm[:, 1:2], warm[:, 0:1], ACT.Sqrt)
            for t, v in enumerate((b1, b2, gamma, beta)):
                act.dma_start(vecs[t * KD:(t + 1) * KD, :], v.rearrange("(k p) -> k p", p=P)).then_inc(s_vec, 16)
            act.dma_start(rw[:, :], router_w[:, :]).then_inc(s_vec, 16)
            for g, (a, b) in enumerate(GROUPS):
                act.wait_ge(s_var, g + 1)
                act.activation(rstd[:, a:b], mv[:, a:b, 1], ACT.Sqrt).then_inc(s_std, 1)
                act.wait_ge(s_shift, g + 1)
                for c in range(a, b):
                    act.activation(xn[:, c, :], x_sb[:, c, :], ACT.Identity, bias=shift[:, c:c + 1],
                                   scale=rstd[:, c:c + 1]).then_inc(s_xn, 1)
                act.wait_ge(s_xn, b)
                if b < NT:
                    act.dma_start(xrows(xn_dram, a, b), xn[:, a:b, :]).then_inc(s_xnd, 16)
                else:
                    act.dma_start(xn_dram[(NT - 1) * P:N, :], xn[0:LASTN, NT - 1, :]).then_inc(s_xnd, 16)
            for i, w in enumerate((W1, W2)):
                act.dma_start(raw[:, i, :].rearrange("p (k d) -> p k d", k=KD), w.rearrange("(k p) d -> p k d", p=P)
                              ).then_inc(s_w12, 16)
            act.wait_ge(s_spanv, 1)
            act.wait_ge(s_w12, 32)
            for i, w in enumerate((W1_h, W2_h)):
                act.copy(w[:, :, :], raw[:, i, :].rearrange("p (k d) -> p k d", k=KD)).then_inc(s_w12h, 1)

            def relu(r, count):
                act.wait_ge(s_sum, count)
                act.activation(ea[:, r, :, :], ea[:, r, :, :], ACT.Relu).then_inc(s_msg, 1)

            with act.Fori(0, NFULL // RING) as i:
                for r in range(RING):
                    relu(r, i * RING + (r + 1))
            relu(0, NSTEP)

            act.wait_ge(s_zero, 5)
            for n in range(SURE, SLOTS):
                act.dma_start(y_dram[n * P:(n + 1) * P, :], y_sb[:, :]).then_inc(s_yst, 16)

            for c in range(NT):
                act.wait_ge(s_tr, c + 1)
                act.copy(hT_h[:, :, c * P:(c + 1) * P],
                         ps[:, 3 + c % 2, :].rearrange("p (k n) -> p k n", k=KD)).then_inc(s_trh, 1)
            for n, (lo, w) in enumerate(CHUNKS):
                for m in range(KD):
                    i = n * KD + m
                    if i >= 2:
                        act.wait_ge(s_ul, i - 1)
                    act.wait_ge(s_l1, i + 1)
                    act.activation(u32[:, i % 2, 0:w], ps[:, 5 + i % 2, 0:w], ACT.Relu,
                                   bias=vecT[:, 0, m:m + 1]).then_inc(s_u, 1)
                    act.wait_ge(s_u, i + 1)
                    act.copy(uT_h[:, n % 2, m, 0:w], u32[:, i % 2, 0:w]).then_inc(s_uh, 1)
            act.wait_ge(s_bvar, 1)
            act.activation(bsc[:, 0, :], bmv[:, :, 1], ACT.Sqrt).then_inc(s_bstd, 1)
            act.wait_ge(s_bsc, 1)
            for half in (0, 1):
                cols = slice(half * HALF * P, (half + 1) * HALF * P)
                for m in range(KD // 2):
                    act.activation(oT[:, m, cols], oT[:, m, cols], ACT.Identity, bias=bsc[:, 2, m:m + 1],
                                   scale=bsc[:, 1, m:m + 1]).then_inc(s_bna, 1)
            for half in (0, 1):
                a, b = half * HALF, (half + 1) * HALF
                act.wait_ge(s_var2, half + 1)
                act.activation(rstd[:, a:b], mv[:, a:b, 1], ACT.Sqrt).then_inc(s_std2, 1)
                act.wait_ge(s_shift2, half + 1)
                for c in range(a, b):
                    act.activation(xn[:, c, :], x_sb[:, c, :], ACT.Identity, bias=shift[:, c:c + 1],
                                   scale=rstd[:, c:c + 1]).then_inc(s_x2, 1)
                act.wait_ge(s_x2, b)
                act.dma_start(xrows(x2_dram, a, b), xn[:, a:b, :]).then_inc(s_x2d, 16)
                if half == 0:
                    for c in range(a, b):
                        act.wait_ge(s_x2t, c + 1)
                        if c >= 2:
                            act.wait_ge(s_log, c - 1)
                        act.copy(x2T[:, c % 2, :, :], ps[:, 3 + c % 2, :].rearrange("p (k n) -> p k n", k=KD)
                                 ).then_inc(s_x2ca, 1)
            act.wait_ge(s_d, 1)
            act.activation(wt[:, 1, :], wt[:, 0, :], ACT.Exp).then_inc(s_ex, 1)

            def part_gu(k, e):
                act.wait_ge(s_raw[k % SRING], 32 * (e * 2 + (k // SRING + 1)))
                act.copy(gu_h[:, k, :], raw[:, k % SRING, :]).then_inc(s_guh, 1)

            def part_dn(c, e):
                r = (GUC + c) % SRING
                act.wait_ge(s_raw[r], 32 * (e * 2 + 2))
                act.copy(dn_h[:, c, :], raw[:, r, :]).then_inc(s_dnh, 1)

            def silu(n):
                act.wait_ge(s_gu, n * GUC + GUC)
                act.activation(hid[:, :], ps[:, 0:2, :].rearrange("p a b -> p (a b)"), ACT.Silu).then_inc(s_sig, 1)

            def rows_high(n):
                act.wait_ge(s_rt, n + 1)
                act.copy(rT_h[:, :, :], ps[:, 7, :].rearrange("p (k n) -> p k n", k=KD)).then_inc(s_rh, 1)

            def hidden_high(n):
                for half in (0, 1):
                    act.wait_ge(s_ht, n * 2 + (half + 1))
                    act.copy(hidT_h[:, half * 4:half * 4 + 4, :],
                             ps[:, 4 + half, :].rearrange("p (k n) -> p k n", k=4)).then_inc(s_hh, 1)

            def store(n):
                act.wait_ge(s_ysb, n + 2)
                act.dma_start(y_dram[bass.ds(n * P, P), :], y_sb[:, :]).then_inc(s_yst, 16)

            for k in range(GUC):
                part_gu(k, 0)
            rows_high(0)
            silu(0)
            rows_high(1)
            for c in range(DC):
                part_dn(c, 0)
            act.wait_ge(s_tab, 1)
            last = act.value_load(last_i[0:1, 0:1], min_val=SURE - 1, max_val=SLOTS - 1)
            with act.Fori(0, last) as j:
                n = row_tile(j)
                m = n + 1
                hidden_high(n)
                changes = act.value_load(tile_v[0:1, 1, bass.ds(m, 1)], min_val=0, max_val=1)
                with act.If(changes):
                    e = act.value_load(tile_v[0:1, 0, bass.ds(m, 1)], min_val=0, max_val=NX - 1) + 1
                    for k in range(GUC - 1):
                        act.wait_ge(s_gu, m * GUC + (k + 1))
                        part_gu(k, e)
                silu(m)
                rows_high(n + 2)
                with act.If(changes):
                    e = act.value_load(tile_v[0:1, 0, bass.ds(m, 1)], min_val=0, max_val=NX - 1) + 1
                    part_gu(GUC - 1, e)
                store(n)
                changed = act.value_load(tile_v[0:1, 1, bass.ds(n, 1)], min_val=0, max_val=1)
                with act.If(changed):
                    e = act.value_load(tile_v[0:1, 0, bass.ds(n, 1)], min_val=0, max_val=NX - 1) + 1
                    for c in range(DC):
                        act.wait_ge(s_y, n * DC + (c + 1))
                        part_dn(c, e)
            hidden_high(last)
            store(last)
            act.wait_ge(s_yst, last * 16 + (16 + FILLS))
            act.sem_inc(s_yall, 1)

        @block.vector
        def _(dve):
            chain = [0]

            def fresh(ins):
                chain[0] += 1
                ins.then_inc(s_dve, 1)

            def settled():
                dve.wait_ge(s_dve, chain[0])

            def link(ins):
                fresh(ins)
                settled()

            fresh(dve.memset(warm[:, :], 1.0))
            fresh(dve.memset(ids_i[:, 0, :], 0))
            settled()
            dve.memset(ids_i[:, 1, :], NOWHERE).then_inc(s_padids, 1)
            dve.memset(x_sb[:, NT - 1, :], 0.0).then_inc(s_padx, 1)
            fresh(dve.memset(first[:, :], 0.0))
            fresh(dve.memset(ps[:, 0, :], 0.0))
            settled()
            dve.sem_inc(s_acc, 1)
            dve.sem_inc(s_seg, J)

            def moments(c):
                fresh(dve.bn_stats(stats[:, c, :], x_sb[:, c, :]))

            def variances(a, b):
                settled()
                for c in range(a, b):
                    fresh(dve.bn_aggr(mv[:, c, :], stats[:, c, :]))
                settled()
                return dve.tensor_scalar(mv[:, a:b, 1], mv[:, a:b, 1], EPS, None, ALU.add)

            def shifts(a, b):
                link(dve.reciprocal(rstd[:, a:b], rstd[:, a:b]))
                return dve.scalar_tensor_tensor(out=shift[:, a:b], in0=mv[:, a:b, 0], scalar=-1.0,
                                                in1=rstd[:, a:b], op0=ALU.mult, op1=ALU.mult)

            for g, (a, b) in enumerate(GROUPS):
                dve.wait_ge(s_xin[g], 16)
                for c in range(a, b):
                    moments(c)
                variances(a, b).then_inc(s_var, 1)
                dve.wait_ge(s_std, g + 1)
                shifts(a, b).then_inc(s_shift, 1)

            dve.wait_ge(s_ids, 64)
            dve.tensor_copy(ids_f[:, :, :], ids_i[:, :, :]).then_inc(s_idf, 1)
            dve.wait_ge(s_idf, 1)
            dve.tensor_reduce(span[:, 0:1], ids_f[:, 1, :], AX.X, ALU.min).then_inc(s_span, 1)
            dve.tensor_reduce(span[:, 1:2], ids_f[:, 1, :], AX.X, ALU.max).then_inc(s_span, 1)
            dve.wait_ge(s_const, 5)
            fresh(dve.tensor_copy(node[:, :], node_i[:, :]))
            fresh(dve.tensor_copy(tok[:, :], tok_i[:, :]))
            fresh(dve.tensor_copy(em8[:, :], em8_i[:, :]))
            dve.wait_ge(s_tps, 1)
            dve.tensor_copy(srcT[:, :, :], ps[:, 4, 0:J * NSTEP].rearrange("p (j g) -> p g j", j=J)
                            ).then_inc(s_idx, 1)
            fresh(dve.tensor_copy(dstT[:, :, :], ps[:, 5, 0:J * NSTEP].rearrange("p (j g) -> p g j", j=J)))
            dve.wait_ge(s_tps, 2)
            link(dve.tensor_copy(span_i[:, :, :], ps[0:1, 6, 0:2 * NSTEP].rearrange("p (t g) -> p t g", t=2)))
            link(dve.tensor_scalar(span_v[:, :, :], span_i[:, :, :], 7, None, ALU.arith_shift_right))
            link(dve.tensor_copy(span_f[:, :, :], span_v[:, :, :]))
            dve.tensor_scalar(span_v[:, :, :], span_f[:, :, :], float(NT - 1), None, ALU.min).then_inc(s_spanv, 1)
            for g, (a, b) in enumerate(GROUPS):
                dve.wait_ge(s_xn, b)
                fresh(dve.tensor_copy(agg[:, a:b, :], xn[:, a:b, :]))
            link(dve.tensor_scalar(valid[:, :], tok[:, :], float(N), None, ALU.is_lt))
            link(dve.tensor_tensor(tok[:, :], tok[:, :], valid[:, :], ALU.mult))
            dve.wait_ge(s_tps, 3)
            fresh(dve.tensor_copy(vecT[:, :, :], ps[:, 7, 0:4 * KD].rearrange("p (t k) -> p t k", t=4)))
            fresh(dve.tensor_copy(rwT[:, :, :], ps[:, 7, 4 * KD:4 * KD + KD * NX].rearrange("p (k e) -> p k e", k=KD)))
            settled()

            def add(r, count):
                dve.wait_ge(s_ea[r], count * 16)
                dve.wait_ge(s_xg[r], count * 16 * J)
                dve.tensor_tensor(ea[:, r, :, :], ea[:, r, :, :], xg[:, r, :, :], ALU.add).then_inc(s_sum, 1)

            unit = dve.alloc_register("unit")
            behind = dve.alloc_register("behind")
            dve.reg_mov(unit, 1)
            dve.reg_mov(behind, 0)

            def accumulate(u):
                k = dve.snap(behind, min_val=0, max_val=NT - 1)
                dve.wait_ge(s_seg, u * J)
                dve.wait_ge(s_acc, u)
                a = agg[:, bass.ds(k, 1), :].rearrange("p a d -> p (a d)")
                b = ps[:, bass.ds((u + 1) % 2, 1), :].rearrange("p a d -> p (a d)")
                dve.tensor_tensor(a, a, b, ALU.add).then_inc(s_acc, 1)

            def segment(g):
                lo, hi = (dve.value_load(span_v[0:1, k, bass.ds(g, 1)], min_val=0, max_val=NT - 1) for k in (0, 1))
                with dve.Fori(lo, hi + 1) as k:
                    u = dve.snap(unit, min_val=1, max_val=NSTEP * NT)
                    for j in range(J):
                        dve.wait_ge(s_seg, u * J - (J - 1) + j)
                        dve.tensor_tensor(onehot[:, j, :], node[:, bass.ds(k * P, P)],
                                          dstT[:, bass.ds(g, 1), j].broadcast_to([P, P]), ALU.is_equal
                                          ).then_inc(s_hot, 1)
                    accumulate(u)
                    dve.reg_mov(behind, k)
                    dve.reg_add(unit, unit, 1)

            for i, (w, h) in enumerate(((W1_l, W1_h), (W2_l, W2_h))):
                dve.wait_ge(s_w12h, i + 1)
                dve.tensor_tensor(w[:, :, :], raw[:, i, :].rearrange("p (k d) -> p k d", k=KD),
                                  h[:, :, :].bitcast(F32), ALU.subtract).then_inc(s_w12l, 1)
            dve.wait_ge(s_spanv, 1)
            add(0, 1)
            with dve.Fori(0, NFULL // RING) as i:
                for r in range(RING):
                    segment(i * RING + r)
                    add((r + 1) % RING, i + 1 + (r + 1) // RING)
            segment(NFULL)
            accumulate(dve.snap(unit, min_val=1, max_val=NSTEP * NT + 1))
            products = dve.snap(unit, min_val=1, max_val=NSTEP * NT + 1)
            dve.wait_ge(s_acc, products + 1)
            dve.sem_inc(s_agg, 1)

            for c in range(NT):
                dve.wait_ge(s_trh, c + 1)
                a = hT_l[:, :, c * P:(c + 1) * P]
                dve.tensor_tensor(a, ps[:, 3 + c % 2, :].rearrange("p (k n) -> p k n", k=KD),
                                  hT_h[:, :, c * P:(c + 1) * P].bitcast(F32), ALU.subtract).then_inc(s_trl, 1)

            def hidden_low(n):
                lo, w = CHUNKS[n]
                for m in range(KD):
                    i = n * KD + m
                    dve.wait_ge(s_uh, i + 1)
                    dve.tensor_tensor(uT_l[:, n % 2, m, 0:w], u32[:, i % 2, 0:w],
                                      uT_h[:, n % 2, m, 0:w].bitcast(F32), ALU.subtract).then_inc(s_ul, 1)

            def second(n):
                lo, w = CHUNKS[n]
                for m in range(KD):
                    i = n * KD + m
                    dve.wait_ge(s_l2, i + 1)
                    dve.tensor_scalar(oT[:, m, lo:lo + w], ps[:, i % 2, 0:w], vecT[:, 1, m:m + 1], None,
                                      ALU.add).then_inc(s_l2c, 1)
                    dve.wait_ge(s_l2c, i + 1)
                    fresh(dve.bn_stats(bst[:, m, n, :], oT[:, m, lo:min(lo + w, N)]))

            hidden_low(0)
            for n in range(1, NC):
                hidden_low(n)
                second(n - 1)
            second(NC - 1)
            settled()
            for m in range(KD):
                fresh(dve.bn_aggr(bmv[:, m, :], bst[:, m, :, :].rearrange("p n s -> p (n s)")))
            settled()
            dve.tensor_scalar(bmv[:, :, 1], bmv[:, :, 1], EPS, None, ALU.add).then_inc(s_bvar, 1)
            dve.wait_ge(s_bstd, 1)
            link(dve.reciprocal(bsc[:, 0, :], bsc[:, 0, :]))
            link(dve.tensor_tensor(bsc[:, 1, :], bsc[:, 0, :], vecT[:, 2, :], ALU.mult))
            link(dve.tensor_tensor(bsc[:, 0, :], bmv[:, :, 0], bsc[:, 1, :], ALU.mult))
            dve.tensor_tensor(bsc[:, 2, :], vecT[:, 3, :], bsc[:, 0, :], ALU.subtract).then_inc(s_bsc, 1)
            dve.wait_ge(s_bsc, 1)
            for half in (0, 1):
                cols = slice(half * HALF * P, (half + 1) * HALF * P)
                for m in range(KD // 2, KD):
                    dve.tensor_scalar(oT[:, m, cols], oT[:, m, cols], bsc[:, 1, m:m + 1], bsc[:, 2, m:m + 1],
                                      ALU.mult, ALU.add).then_inc(s_bnd, 1)

            for half in (0, 1):
                a, b = half * HALF, (half + 1) * HALF
                for c in range(a, b):
                    dve.wait_ge(s_oTt, c + 1)
                    dve.tensor_tensor(x_sb[:, c, :], x_sb[:, c, :], ps[:, c % 2, :], ALU.add).then_inc(s_x1, 1)
                    dve.wait_ge(s_x1, c + 1)
                    moments(c)
                variances(a, b).then_inc(s_var2, 1)
                dve.wait_ge(s_std2, half + 1)
                shifts(a, b).then_inc(s_shift2, 1)
            for c in range(HALF, NT):
                dve.wait_ge(s_x2t, c + 1)
                dve.wait_ge(s_log, c - 1)
                dve.tensor_copy(x2T[:, c % 2, :, :], ps[:, 3 + c % 2, :].rearrange("p (k n) -> p k n", k=KD)
                                ).then_inc(s_x2cd, 1)

            def spread(v):
                return v.unsqueeze(2).broadcast_to([P, NT, NX])

            em8_b = em8[:, :].unsqueeze(1).broadcast_to([P, NT, NX])
            dve.wait_ge(s_log, NT)
            link(dve.tensor_copy(L[:, :, :], ps[:, 2, 0:NT * NX].rearrange("p (c e) -> p c e", e=NX)))
            for k, (logit, mask) in enumerate(((L, M1), (L2, M2))):
                link(dve.tensor_reduce(v12[:, k, :], logit[:, :, :], AX.X, ALU.max))
                link(dve.tensor_tensor(t8[:, :, :], logit[:, :, :], spread(v12[:, k, :]), ALU.is_equal))
                link(dve.tensor_tensor(t8[:, :, :], t8[:, :, :], em8_b, ALU.mult))
                link(dve.tensor_reduce(i12[:, k, :], t8[:, :, :], AX.X, ALU.min))
                link(dve.tensor_tensor(mask[:, :, :], em8_b, spread(i12[:, k, :]), ALU.is_equal))
                if k == 0:
                    link(dve.scalar_tensor_tensor(out=L2[:, :, :], in0=M1[:, :, :], scalar=FAR, in1=L[:, :, :],
                                                  op0=ALU.mult, op1=ALU.add))
            dve.tensor_tensor(wt[:, 0, :], v12[:, 1, :], v12[:, 0, :], ALU.subtract).then_inc(s_d, 1)
            fresh(dve.tensor_tensor(M1[:, :, :], M1[:, :, :], spread(valid[:, :]), ALU.mult))
            fresh(dve.tensor_tensor(M2[:, :, :], M2[:, :, :], spread(valid[:, :]), ALU.mult))
            settled()
            dve.tensor_tensor(M[:, :, :], M1[:, :, :], M2[:, :, :], ALU.add).then_inc(s_M, 1)

            dve.wait_ge(s_rank, 1)
            link(dve.tensor_scalar(cnt_i[:, 0, :], ps[:, 1, 0:NX], float(P - 1), None, ALU.add))
            link(dve.tensor_scalar(cnt_i[:, 1, :], cnt_i[:, 0, :], 7, None, ALU.arith_shift_right))
            link(dve.tensor_scalar(tiles[:, :], cnt_i[:, 1, :], 1.0, None, ALU.max))
            for e in range(NX):
                link(dve.tensor_tensor(first[:, e + 1:e + 2], first[:, e:e + 1], tiles[:, e:e + 1], ALU.add))
            link(dve.scalar_tensor_tensor(out=t8[:, :, :],
                                          in0=first[:, 0:NX].unsqueeze(1).broadcast_to([P, NT, NX]), scalar=float(P),
                                          in1=ps[:, 0, 0:NT * NX].rearrange("p (c e) -> p c e", e=NX),
                                          op0=ALU.mult, op1=ALU.add))
            fresh(dve.tensor_tensor(t9[:, :, :], t8[:, :, :], M1[:, :, :], ALU.mult))
            fresh(dve.tensor_tensor(L2[:, :, :], t8[:, :, :], M2[:, :, :], ALU.mult))
            settled()
            fresh(dve.tensor_reduce(pos[:, 0, :], t9[:, :, :], AX.X, ALU.add))
            fresh(dve.tensor_reduce(pos[:, 1, :], L2[:, :, :], AX.X, ALU.add))
            settled()
            link(dve.tensor_copy(pos_i[:, :, :], pos[:, :, :]))
            flat = pos_i[:, :, :].rearrange("p k c -> p (k c)")
            fresh(dve.tensor_scalar(ps_i[:, 0, :], flat, P - 1, None, ALU.bitwise_and))
            fresh(dve.tensor_scalar(ps_i[:, 1, :], flat, 7, None, ALU.arith_shift_right))
            settled()
            link(dve.tensor_copy(ps_f[:, :, :], ps_i[:, :, :]))
            link(dve.tensor_tensor(slotB[:, :, :], node[:, 0:SLOTS].unsqueeze(1).broadcast_to([P, 2 * NT, SLOTS]),
                                   ps_f[:, 1, :].unsqueeze(2).broadcast_to([P, 2 * NT, SLOTS]), ALU.is_equal))
            for k in (0, 1):
                part = slice(k * NT, (k + 1) * NT)
                fresh(dve.tensor_tensor(slotB[:, part, :], slotB[:, part, :],
                                        tok[:, :].unsqueeze(2).broadcast_to([P, NT, SLOTS]), ALU.mult))
                settled()
                dve.tensor_tensor(hot[:, part, :], node[:, 0:P].unsqueeze(1).broadcast_to([P, NT, P]),
                                  ps_f[:, 0, part].unsqueeze(2).broadcast_to([P, NT, P]), ALU.is_equal
                                  ).then_inc(s_hotr, 1)
            dve.wait_ge(s_slot, 1)
            dve.tensor_copy(slot_i[:, 0:SLOTS], ps[:, 2, 0:SLOTS]).then_inc(s_sloti, 1)
            starts = first[0:1, 1:NX].unsqueeze(1).broadcast_to([1, SLOTS, NX - 1])
            fresh(dve.tensor_tensor(cmp7[:, 0, :, :], node[0:1, 0:SLOTS].unsqueeze(2).broadcast_to([1, SLOTS, NX - 1]),
                                    starts, ALU.is_ge))
            fresh(dve.tensor_tensor(cmp7[:, 1, :, :],
                                    node[0:1, 1:SLOTS + 1].unsqueeze(2).broadcast_to([1, SLOTS, NX - 1]),
                                    starts, ALU.is_equal))
            settled()
            link(dve.tensor_reduce(tile_f[:, :, :], cmp7[:, :, :, :], AX.X, ALU.add))
            fresh(dve.tensor_copy(tile_v[:, :, :], tile_f[:, :, :]))
            fresh(dve.tensor_scalar(last_i[:, :], first[0:1, NX:NX + 1], -1.0, None, ALU.add))
            settled()
            dve.sem_inc(s_tab, 1)
            dve.wait_ge(s_ex, 1)
            link(dve.tensor_scalar(wt[:, 2, :], wt[:, 1, :], 1.0, None, ALU.add))
            link(dve.reciprocal(w12[:, 0, :], wt[:, 2, :]))
            link(dve.tensor_tensor(w12[:, 1, :], wt[:, 1, :], w12[:, 0, :], ALU.mult))

            def part_gu(k, e):
                dve.wait_ge(s_guh, e * GUC + (k + 1))
                dve.tensor_tensor(gu_l[:, k, :], raw[:, k % SRING, :], gu_h[:, k, :].bitcast(F32),
                                  ALU.subtract).then_inc(s_gul, 1)

            def part_dn(c, e):
                dve.wait_ge(s_dnh, e * DC + (c + 1))
                dve.tensor_tensor(dn_l[:, c, :], raw[:, (GUC + c) % SRING, :], dn_h[:, c, :].bitcast(F32),
                                  ALU.subtract).then_inc(s_dnl, 1)

            def row_copy(n):
                if not isinstance(n, int) or n:
                    dve.wait_ge(s_rt, n)
                dve.wait_ge(s_rrdy, n + 1)
                dve.tensor_scalar(row_cur[:, :], rows[:, bass.ds(n % RROWS, 1), :].rearrange("p a d -> p (a d)"),
                                  1.0, None, ALU.mult).then_inc(s_rcur, 1)

            def rows_low(n):
                dve.wait_ge(s_rh, n + 1)
                dve.tensor_tensor(rT_l[:, :, :], ps[:, 7, :].rearrange("p (k n) -> p k n", k=KD),
                                  rT_h[:, :, :].bitcast(F32), ALU.subtract).then_inc(s_rl, 1)

            def multiply(n):
                dve.wait_ge(s_sig, n + 1)
                dve.tensor_tensor(hid[:, :], hid[:, :], ps[:, 2:4, :].rearrange("p a b -> p (a b)"), ALU.mult
                                  ).then_inc(s_hid, 1)

            def hidden_low_part(n):
                for half in (0, 1):
                    dve.wait_ge(s_hh, n * 2 + (half + 1))
                    a = slice(half * 4, half * 4 + 4)
                    dve.tensor_tensor(hidT_l[:, a, :], ps[:, 4 + half, :].rearrange("p (k n) -> p k n", k=4),
                                      hidT_h[:, a, :].bitcast(F32), ALU.subtract).then_inc(s_hl, 1)

            def result(n):
                dve.wait_ge(s_yst, n * 16 + FILLS)
                dve.wait_ge(s_y, n * DC + DC)
                dve.tensor_copy(y_sb[:, :], ps[:, 6, :]).then_inc(s_ysb, 1)

            dve.wait_ge(s_yst, FILLS)
            dve.sem_inc(s_ysb, 1)
            part_gu(0, 0)
            row_copy(0)
            part_gu(1, 0)
            rows_low(0)
            row_copy(1)
            part_gu(2, 0)
            part_gu(3, 0)
            multiply(0)
            rows_low(1)
            for c in range(DC):
                part_dn(c, 0)
            last = dve.value_load(last_i[0:1, 0:1], min_val=SURE - 1, max_val=SLOTS - 1)
            with dve.Fori(0, last) as j:
                n = row_tile(j)
                m = n + 1
                hidden_low_part(n)
                row_copy(n + 2)
                changes = dve.value_load(tile_v[0:1, 1, bass.ds(m, 1)], min_val=0, max_val=1)
                with dve.If(changes):
                    e = dve.value_load(tile_v[0:1, 0, bass.ds(m, 1)], min_val=0, max_val=NX - 1) + 1
                    for k in range(GUC - 1):
                        part_gu(k, e)
                multiply(m)
                rows_low(n + 2)
                with dve.If(changes):
                    e = dve.value_load(tile_v[0:1, 0, bass.ds(m, 1)], min_val=0, max_val=NX - 1) + 1
                    part_gu(GUC - 1, e)
                result(n)
                changed = dve.value_load(tile_v[0:1, 1, bass.ds(n, 1)], min_val=0, max_val=1)
                with dve.If(changed):
                    e = dve.value_load(tile_v[0:1, 0, bass.ds(n, 1)], min_val=0, max_val=NX - 1) + 1
                    for c in range(DC):
                        part_dn(c, e)
            hidden_low_part(last)
            result(last)

            for c in range(NT):
                dve.wait_ge(s_yg[c], 32)
                for k in (0, 1):
                    ins = dve.scalar_tensor_tensor(out=x_sb[:, c, :], in0=yg[:, k, c, :], scalar=w12[:, k, c:c + 1],
                                                   in1=x_sb[:, c, :], op0=ALU.mult, op1=ALU.add)
                    if k == 0:
                        link(ins)
                    else:
                        ins.then_inc(s_out, 1)

        @block.tensor
        def _(pe):
            def turn(bank, c0, source, parts=P):
                cols = source.shape[-1]
                return pe.transpose(ps[0:cols, bank, c0:c0 + parts], source, ident[0:parts, 0:parts])

            def three(outs, left, right, first, last):
                lh, ll = left
                for o, (rh, rl) in zip(outs, right):
                    pe.matmul(o, lh, rh, start=first, stop=False, skip_group_check=True)
                for o, (rh, rl) in zip(outs, right):
                    pe.matmul(o, lh, rl, start=False, stop=False, skip_group_check=True)
                for o, (rh, rl) in zip(outs, right):
                    ins = pe.matmul(o, ll, rh, start=False, stop=last, skip_group_check=True)
                return ins

            pe.wait_ge(s_const, 2)
            pe.wait_ge(s_idf, 1)
            for t, bank in ((0, 4), (1, 5)):
                for j in range(J):
                    last = turn(bank, j * NSTEP, ids_f[:, t, :].rearrange("g (p j) -> g j p", j=J)[:, j, :], NSTEP)
            last.then_inc(s_tps, 1)
            pe.wait_ge(s_span, 2)
            for t in (0, 1):
                last = turn(6, t * NSTEP, span[:, t:t + 1], NSTEP)
            last.then_inc(s_tps, 1)
            pe.wait_ge(s_vec, 80)
            turn(7, 0, vecs[:, :], 4 * KD)
            for k in range(KD):
                last = turn(7, 4 * KD + k * NX, rw[:, k * P:(k + 1) * P], NX)
            last.then_inc(s_tps, 1)

            unit = pe.alloc_register("unit")
            pe.reg_mov(unit, 1)

            def segment(g, r, count):
                lo, hi = (pe.value_load(span_v[0:1, k, bass.ds(g, 1)], min_val=0, max_val=NT - 1) for k in (0, 1))
                with pe.Fori(lo, hi + 1) as k:
                    u = pe.snap(unit, min_val=1, max_val=NSTEP * NT)
                    pe.wait_ge(s_msg, count)
                    pe.wait_ge(s_acc, u)
                    acc = ps[:, bass.ds(u % 2, 1), :].rearrange("p a d -> p (a d)")
                    for j in range(J):
                        pe.wait_ge(s_hot, u * J - (J - 1) + j)
                        pe.matmul(acc, onehot[:, j, :], ea[:, r, j, :], start=(j == 0), stop=(j == J - 1)
                                  ).then_inc(s_seg, 1)
                    pe.reg_add(unit, unit, 1)
                pe.matmul(ps[:, 2, 0:1], ident[:, :], ident[:, 0:1], start=True, stop=True).then_inc(s_step, 1)

            pe.wait_ge(s_spanv, 1)
            with pe.Fori(0, NFULL // RING) as i:
                for r in range(RING):
                    segment(i * RING + r, r, i * RING + (r + 1))
            segment(NFULL, 0, NSTEP)

            pe.wait_ge(s_agg, 1)
            for c in range(NT):
                if c >= 2:
                    pe.wait_ge(s_trl, c - 1)
                for k in range(KD):
                    last = turn(3 + c % 2, k * P, agg[:, c, k * P:(k + 1) * P])
                last.then_inc(s_tr, 1)
            pe.wait_ge(s_w12l, 2)

            def first_layer(n):
                lo, w = CHUNKS[n]
                pe.wait_ge(s_trl, (lo + w) // P)
                for m in range(KD):
                    i = n * KD + m
                    if i >= 2:
                        pe.wait_ge(s_u, i - 1)
                    for k in range(KD):
                        cols = slice(m * P, (m + 1) * P)
                        last = three([ps[:, 5 + i % 2, 0:w]], (W1_h[:, k, cols], W1_l[:, k, cols]),
                                     [(hT_h[:, k, lo:lo + w], hT_l[:, k, lo:lo + w])], k == 0, k == KD - 1)
                    last.then_inc(s_l1, 1)

            def second_layer(n):
                lo, w = CHUNKS[n]
                pe.wait_ge(s_ul, (n + 1) * KD)
                for m in range(KD):
                    i = n * KD + m
                    if i >= 2:
                        pe.wait_ge(s_l2c, i - 1)
                    cols = slice(m * P, (m + 1) * P)
                    for c in range(lo // P, (lo + w) // P):
                        a = c * P - lo
                        pe.matmul(ps[:, i % 2, a:a + P], xn[:, c, cols], ident[:, :],
                                  start=(a == 0), stop=False, skip_group_check=True)
                    for k in range(KD):
                        last = three([ps[:, i % 2, 0:w]], (W2_h[:, k, cols], W2_l[:, k, cols]),
                                     [(uT_h[:, n % 2, k, 0:w], uT_l[:, n % 2, k, 0:w])], False, k == KD - 1)
                    last.then_inc(s_l2, 1)

            first_layer(0)
            for n in range(1, NC):
                first_layer(n)
                second_layer(n - 1)
            second_layer(NC - 1)

            for c in range(NT):
                if c % HALF == 0:
                    pe.wait_ge(s_bna, (c // HALF + 1) * KD // 2)
                    pe.wait_ge(s_bnd, (c // HALF + 1) * KD // 2)
                if c >= 2:
                    pe.wait_ge(s_x1, c - 1)
                for m in range(KD):
                    last = turn(c % 2, m * P, oT[:, m, c * P:(c + 1) * P])
                last.then_inc(s_oTt, 1)

            def turn_token(c):
                pe.wait_ge(s_x2, c + 1)
                for k in range(KD):
                    last = turn(3 + c % 2, k * P, xn[:, c, k * P:(k + 1) * P])
                last.then_inc(s_x2t, 1)

            turn_token(0)
            for c in range(NT):
                if c + 1 < NT:
                    turn_token(c + 1)
                if c < HALF:
                    pe.wait_ge(s_x2ca, c + 1)
                else:
                    pe.wait_ge(s_x2cd, c - HALF + 1)
                for k in range(KD):
                    last = pe.matmul(ps[:, 2, c * NX:(c + 1) * NX], x2T[:, c % 2, k, :], rwT[:, k, :],
                                     start=(k == 0), stop=(k == KD - 1))
                last.then_inc(s_log, 1)
            pe.wait_ge(s_M, 1)
            Mf = M[:, :, :].rearrange("p c e -> p (c e)")
            pe.matmul(ps[:, 0, 0:NT * NX], before[:, :], Mf, start=True, stop=False, skip_group_check=True)
            for d in range(1, NT):
                pe.matmul(ps[:, 0, d * NX:NT * NX], ones[:, :], Mf[:, 0:(NT - d) * NX],
                          start=False, stop=(d == NT - 1), skip_group_check=True)
            for c in range(NT):
                last = pe.matmul(ps[:, 1, 0:NX], ones[:, :], M[:, c, :], start=(c == 0), stop=(c == NT - 1))
            last.then_inc(s_rank, 1)
            for t in range(2 * NT):
                if t % NT == 0:
                    pe.wait_ge(s_hotr, t // NT + 1)
                last = pe.matmul(ps[:, 2, 0:SLOTS], hot[:, t, :], slotB[:, t, :], start=(t == 0), stop=(t == 2 * NT - 1))
            last.then_inc(s_slot, 1)

            def turn_rows(n):
                pe.wait_ge(s_rcur, n + 1)
                for k in range(KD):
                    last = turn(7, k * P, row_cur[:, k * P:(k + 1) * P])
                last.then_inc(s_rt, 1)

            def gate_up(n, e):
                pe.wait_ge(s_rl, n + 1)
                for k in range(KD):
                    pe.wait_ge(s_gul, e * GUC + (k + 1))
                    halves = [slice(b * BANK, (b + 1) * BANK) for b in range(PIECE // BANK)]
                    three([ps[:, b, :] for b in range(PIECE // BANK)], (rT_h[:, k, :], rT_l[:, k, :]),
                          [(gu_h[:, k, a], gu_l[:, k, a]) for a in halves], k == 0, k == KD - 1).then_inc(s_gu, 1)

            def turn_hidden(n):
                pe.wait_ge(s_hid, n + 1)
                for half in (0, 1):
                    for k in range(4):
                        a = (half * 4 + k) * P
                        last = turn(4 + half, k * P, hid[:, a:a + P])
                    last.then_inc(s_ht, 1)

            def down(n, e):
                pe.wait_ge(s_ysb, n + 1)
                kk = KH // DC
                for c in range(DC):
                    pe.wait_ge(s_dnl, e * DC + (c + 1))
                    pe.wait_ge(s_hl, n * 2 + (c + 1))
                    for i in range(kk):
                        k = c * kk + i
                        a = slice(i * D, (i + 1) * D)
                        last = three([ps[:, 6, :]], (hidT_h[:, k, :], hidT_l[:, k, :]),
                                     [(dn_h[:, c, a], dn_l[:, c, a])], k == 0, k == KH - 1)
                    last.then_inc(s_y, 1)

            def expert_of(n):
                return pe.value_load(tile_v[0:1, 0, bass.ds(n, 1)], min_val=0, max_val=NX - 1)

            turn_rows(0)
            gate_up(0, 0)
            turn_rows(1)
            pe.wait_ge(s_tab, 1)
            last = pe.value_load(last_i[0:1, 0:1], min_val=SURE - 1, max_val=SLOTS - 1)
            with pe.Fori(0, last) as j:
                n = row_tile(j)
                turn_hidden(n)
                gate_up(n + 1, expert_of(n + 1))
                turn_rows(n + 2)
                down(n, expert_of(n))
            turn_hidden(last)
            down(last, NX - 1)


_INS = ['x', 'src', 'dst', 'edge_attr_512', 'L0_gnn_W1', 'L0_gnn_b1', 'L0_gnn_W2', 'L0_gnn_b2', 'L0_gnn_gamma',
        'L0_gnn_beta', 'L0_ffn_router_w', 'L0_ffn_w_gate', 'L0_ffn_w_up', 'L0_ffn_w_down']


def kernel(**inputs):
    import numpy as _np
    import concourse.bacc as _bacc
    from concourse import mybir as _mybir
    from concourse.bass_utils import run_bass_kernel_spmd as _run

    nc = _bacc.Bacc("TRN2", target_bir_lowering=False, num_devices=1)
    arrays, args = {}, []
    for name in _INS:
        a = _np.ascontiguousarray(inputs[name])
        arrays[f"in_{name}_dram"] = a
        args.append(nc.dram_tensor(f"in_{name}_dram", a.shape, _mybir.dt.from_np(a.dtype), kind="ExternalInput").ap())
    out = nc.dram_tensor("out_0_dram", inputs["x"].shape, _mybir.dt.from_np(_np.dtype("float32")),
                         kind="ExternalOutput").ap()
    gnn_moe_program(nc, *args, out)
    r = _run(nc, [arrays], core_ids=[0])
    return r.results[0]["out_0_dram"]
```

```python
from contextlib import ExitStack

import concourse.bass as bass
from concourse import mybir

F32 = mybir.dt.float32
F32R = mybir.dt.float32r
F16 = mybir.dt.float16
I32 = mybir.dt.int32
ALU = mybir.AluOpType
ACT = mybir.ActivationFunctionType
AX = mybir.AxisListType

P = 128
BANK = 512
EPS = 1e-5
FAR = -3.0e38


def gnn_moe_program(nc, x, src, dst, edge_attr, W1, b1, W2, b2, gamma, beta,
                    router_w, w_gate, w_up, w_down, out):
    N, D = x.shape
    E = src.shape[0]
    NX, _, H = w_gate.shape
    NT = -(-N // P)
    LASTN = N - (NT - 1) * P
    NP = NT * P
    KD, KH = D // P, H // P
    J = 4
    STEP = P * J
    NFULL = E // STEP
    TAILP = E - NFULL * STEP
    NSTEP = NFULL + 1
    RING = 5
    ROUNDS = NSTEP // RING
    assert NSTEP % RING == 0 and 0 < TAILP <= P
    SLOTS = (2 * N + NX * P) // P
    SURE = -(-2 * N // P)
    CHUNKS = [(0, BANK), (BANK, BANK), (2 * BANK, NP - 2 * BANK)]
    NC = len(CHUNKS)
    EARLY = CHUNKS[0][1] // P
    LATER = [(EARLY + (NT - EARLY) * m // (KD - 1), EARLY + (NT - EARLY) * (m + 1) // (KD - 1))
             for m in range(KD - 1)]
    TURNED = (3, 4, 7, 2)
    NOWHERE = 2048
    GROUPS = [(0, 3), (3, 6), (6, 9), (9, NT)]
    HALF = NT // 2
    GUC, DC = KD, 2
    PIECE = 2 * H
    SRING = 3
    X1_BANKS, X2_BANKS = (0, 1, 5), (3, 4, 7)
    X2_DVE = range(HALF, HALF + 3)
    X2T_ACT = (0, 1, 2, 3, 6, 8)
    X2T_DVE = [c for c in range(NT) if c not in X2T_ACT]
    RROWS = 8
    assert H == 2 * BANK
    assert (GUC + DC) % SRING == 0 and PIECE == KH // DC * D

    xn_dram = nc.dram_tensor("xn_rows", [N, D], F32, kind="Internal").ap()
    x2_dram = nc.dram_tensor("x2_rows", [NP, D], F32, kind="Internal").ap()
    sum_dram = nc.dram_tensor("sum_rows", [NP + P, D], F32, kind="Internal").ap()

    with ExitStack() as ctx:
        def sb(name, shape, dt=F32):
            return ctx.enter_context(nc.sbuf_tensor(name, shape, dt))

        def sem(name):
            return ctx.enter_context(nc.semaphore(name))

        KB = 1024
        base = -(-nc.sbuf_base // 64) * 64
        O_XN, O_AGG, O_RAW, O_G = 20 * KB, 40 * KB, 60 * KB, 84 * KB
        ctx.enter_context(nc.sbuf_tensor("arena", [P, 188 * KB + 64], mybir.dt.uint8))

        def at(name, offset, shape, dt=F32):
            return nc.alloc_sbuf_tensor_at(name, [P, *shape], dt, offset=base + offset)

        x_sb = at("x_sb", 0, [NT, D])
        xn = at("xn", O_XN, [NT, D])
        rT_h, rT_l = (at(f"rT_{c}", O_XN + i * 2 * KB, [KD, P], F32R) for i, c in enumerate("hl"))
        hid = at("hid", O_XN + 4 * KB, [H])
        hidT_h, hidT_l = (at(f"hidT_{c}", O_XN + (8 + 4 * i) * KB, [KH, P], F32R) for i, c in enumerate("hl"))
        row_cur = at("row_cur", O_XN + 16 * KB, [D])
        xnT = at("xnT", O_XN, [NT, KD, P])
        agg = at("agg", O_AGG, [NT, D])
        oT = at("oT", O_AGG, [KD, NP])
        rows = at("rows", O_AGG, [RROWS, D])
        raw = at("raw", O_RAW, [SRING, PIECE])
        u32 = raw[:, 2, 0:2 * BANK].rearrange("p (r n) -> p r n", r=2)
        ea = at("ea", O_G, [RING, J, D])
        xg = at("xg", O_G + 40 * KB, [RING, J, D])
        hT_h, hT_l = (at(f"hT_{c}", O_G + i * 20 * KB, [KD, NP], F32R) for i, c in enumerate("hl"))
        uT_h, uT_l = (at(f"uT_{c}", O_G + (40 + 16 * i) * KB, [2, KD, BANK], F32R) for i, c in enumerate("hl"))
        ids_i = nc.alloc_sbuf_tensor_at("ids_i", [NSTEP, 2, STEP], I32, offset=base + O_G + 80 * KB)
        ids_f = nc.alloc_sbuf_tensor_at("ids_f", [NSTEP, 2, STEP], F32, offset=base + O_G + 84 * KB)
        node_i = at("node_i", O_G + 88 * KB, [NP], I32)
        W1_h, W2_h, W2_l = (at(n, O_G + (80 + 8 * i) * KB, [KD, D], F32R)
                            for i, n in enumerate(("W1_h", "W2_h", "W2_l")))
        W1_l = at("W1_l", O_RAW, [KD, D], F32R)
        x2T = at("x2T", O_G + 56 * KB, [4, KD, P])
        hot = at("hot", O_G + 72 * KB, [2 * NT, P], F16)
        slotE = at("slotE", O_G + 77 * KB, [2 * NT, SLOTS], F16)
        slotB = at("slotB", O_AGG + 8 * KB, [2 * NT, SLOTS], F16)
        cmp7 = at("cmp7", O_AGG + 19 * KB + KB // 4, [2, SLOTS, NX - 1], F16)[0:1]
        slotW = at("slotW", O_AGG + 16 * KB, [2 * NT, 3, SLOTS], F16)
        def pieces(name, *places):
            return [at(f"{name}{i}", O_G + k * KB, [PIECE], F32R) for i, k in enumerate(places)]

        gu_h, gu_l = pieces("gu_h", 0, 8, 16, 40), pieces("gu_l", 24, 32, 80, 48)
        dn_h, dn_l = pieces("dn_h", 56, 64), pieces("dn_l", 88, 96)

        y_sb = sb("y_sb", [P, D])
        ident = sb("ident", [P, P])
        before = sb("before", [P, P], F16)
        ones = sb("ones", [P, P], F16)
        node = sb("node", [P, NP], F16)
        onehot = sb("onehot", [P, J, P])
        tok_i = sb("tok_i", [P, NT], I32)
        tok = sb("tok", [P, NT])
        valid = sb("valid", [P, NT])
        mv = sb("mv", [P, NT, 2])
        rstd = sb("rstd", [P, NT])
        shift = sb("shift", [P, NT])
        stats = sb("stats", [P, NT, 6])
        dstT = sb("dstT", [P, NSTEP, J])
        srcT = sb("srcT", [P, NSTEP, J], I32)
        idx = sb("idx", [P, RING, J], I32)
        span = sb("span", [NSTEP, 2])
        span_i = sb("span_i", [1, 2, NSTEP], I32)
        span_f = sb("span_f", [1, 2, NSTEP])
        span_v = sb("span_v", [1, 2, NSTEP], I32)
        vecs = sb("vecs", [4 * KD, P])
        vecT = sb("vecT", [P, 4, KD])
        rw = sb("rw", [NX, D])
        rwT = sb("rwT", [P, KD, NX])
        bst = sb("bst", [P, KD, NC, 6])
        bmv = sb("bmv", [P, KD, 2])
        bsc = sb("bsc", [P, 3, KD])
        em8_i = sb("em8_i", [P, NX], I32)
        em8 = sb("em8", [P, NX])
        L = sb("L", [P, NT, NX])
        L2 = sb("L2", [P, NT, NX])
        t8 = sb("t8", [P, NT, NX])
        t9 = sb("t9", [P, NT, NX])
        M1 = sb("M1", [P, NT, NX])
        M2 = sb("M2", [P, NT, NX])
        M = sb("M", [P, NT, NX], F16)
        cnt = sb("cnt", [P, NX])
        v12 = sb("v12", [P, 2, NT])
        i12 = sb("i12", [P, 2, NT])
        w12 = sb("w12", [P, 2, NT])
        wt = sb("wt", [P, 3, NT])
        cnt_i = sb("cnt_i", [P, 2, NX], I32)
        tiles = sb("tiles", [P, NX])
        first = sb("first", [P, NX + 1])
        last_i = sb("last_i", [1, 1], I32)
        tile_f = sb("tile_f", [1, 5, SLOTS])
        tile_v = sb("tile_v", [1, 5, SLOTS], I32)
        pos = sb("pos", [P, 2, NT])
        pos_i = sb("pos_i", [P, 2, NT], I32)
        ps_i = sb("ps_i", [P, 2, 2 * NT], I32)
        ps_f = sb("ps_f", [P, 2, 2 * NT])
        slot_i = sb("slot_i", [P, SLOTS + 1], I32)
        warm = sb("warm", [1, 2])
        tok1 = sb("tok1", [P, NT])
        nobody = sb("nobody", [P, 1])
        unused = sb("unused", [P, SLOTS])
        target = sb("target", [P, SLOTS], I32)
        w_rest = sb("w_rest", [P, 2, 2 * NT])
        w_part = sb("w_part", [P, 3, 2 * NT], F16)
        w_sum = sb("w_sum", [P, SLOTS])
        w_slot = sb("w_slot", [P, SLOTS])

        ps = ctx.enter_context(nc.psum_tensor("ps", [P, 8, BANK], F32))

        def sems(names):
            return [sem(n) for n in names.split()]

        s_const, s_padx, s_padids, s_zero = sems("s_const s_padx s_padids s_zero")
        s_xin = [sem(f"s_xin{g}") for g in range(len(GROUPS))]
        s_var, s_std, s_shift, s_xna, s_xnv, s_xnd = sems("s_var s_std s_shift s_xna s_xnv s_xnd")
        s_agg0, s_xnt, s_xntc = sems("s_agg0 s_xnt s_xntc")
        s_ids, s_idf, s_span, s_tps, s_idx, s_spanv = sems("s_ids s_idf s_span s_tps s_idx s_spanv")
        s_vec, s_w12h, s_w12l, s_dve = sems("s_vec s_w12h s_w12l s_dve")
        s_w12 = [sem(f"s_w{i}") for i in (1, 2)]
        s_ea = [sem(f"s_ea{r}") for r in range(RING)]
        s_xg = [sem(f"s_xg{r}") for r in range(RING)]
        s_idxc, s_idxr, s_sum, s_msg, s_step = sems("s_idxc s_idxr s_sum s_msg s_step")
        s_hot, s_seg, s_acc, s_agg = sems("s_hot s_seg s_acc s_agg")
        s_tr, s_trh, s_trl = sems("s_tr s_trh s_trl")
        s_l1, s_u, s_uh, s_ul, s_l2, s_l2c = sems("s_l1 s_u s_uh s_ul s_l2 s_l2c")
        s_bvar, s_bstd, s_bsc, s_bna, s_bnd = sems("s_bvar s_bstd s_bsc s_bna s_bnd")
        s_oTt, s_x1, s_var2, s_std2, s_shift2 = sems("s_oTt s_x1 s_var2 s_std2 s_shift2")
        s_x2a, s_x2v, s_x2d = sems("s_x2a s_x2v s_x2d")
        s_x2t, s_x2ca, s_x2cv, s_log = sems("s_x2t s_x2ca s_x2cv s_log")
        s_d, s_ex, s_M, s_rank = sems("s_d s_ex s_M s_rank")
        s_tab, s_hotr, s_slot, s_sloti = sems("s_tab s_hotr s_slot s_sloti")
        s_rows, s_rrdy, s_rcur, s_rt, s_rh, s_rl = sems("s_rows s_rrdy s_rcur s_rt s_rh s_rl")
        s_raw = [sem(f"s_raw{r}") for r in range(SRING)]
        s_guh, s_gul, s_dnh, s_dnl = sems("s_guh s_gul s_dnh s_dnl")
        s_gu, s_sig, s_hid, s_ht, s_hh, s_hl = sems("s_gu s_sig s_hid s_ht s_hh s_hl")
        s_y, s_ysb, s_sum0, s_added, s_all, s_outd = sems("s_y s_ysb s_sum0 s_added s_all s_outd")
        s_target, s_wparts, s_wslot = sems("s_target s_wparts s_wslot")

        block = ctx.enter_context(nc.Block())

        def xrows(ap, a, b):
            return ap[a * P:b * P, :].rearrange("(c p) d -> p c d", p=P)

        def row_tile(n):
            return nc.s_assert_within(n, 0, SLOTS, skip_runtime_bounds_check_because="at most SLOTS tiles")

        def flag(engine, row, n):
            n = bass.ds(n, 1) if not isinstance(n, int) else slice(n, n + 1)
            return engine.value_load(tile_v[0:1, row, n], min_val=0, max_val=1)

        def next_expert(engine, n):
            n = bass.ds(n, 1) if not isinstance(n, int) else slice(n, n + 1)
            return engine.value_load(tile_v[0:1, 0, n], min_val=0, max_val=NX - 1) + 1

        def normed(engine, g, b):
            engine.wait_ge(s_xna, g + 1)
            engine.wait_ge(s_xnv, b - (g + 1))

        @block.sync
        def _(sp):
            for g, (a, b) in enumerate(GROUPS):
                if b < NT:
                    sp.dma_start(x_sb[:, a:b, :], xrows(x, a, b)).then_inc(s_xin[g], 16)
                else:
                    sp.wait_ge(s_padx, 1)
                    sp.dma_start(x_sb[0:LASTN, NT - 1, :], x[(NT - 1) * P:N, :]).then_inc(s_xin[g], 16)
            sp.wait_ge(s_ids, 64)

            def load_edges(g, r):
                sp.dma_start(ea[:, r, :, :],
                             edge_attr[bass.ds(g * STEP, STEP), :].rearrange("(p j) d -> p j d", j=J)
                             ).then_inc(s_ea[r], 16)

            AHEAD = 2
            for r in range(RING):
                if r == AHEAD:
                    sp.wait_ge(s_xnd, 16 * len(GROUPS))
                load_edges(r, r)
            with sp.Fori(1, ROUNDS - 1) as i:
                for r in range(RING):
                    g = i * RING + r
                    sp.wait_ge(s_step, g - RING + 1)
                    load_edges(g, r)
            for r in range(RING):
                g = NSTEP - RING + r
                sp.wait_ge(s_step, g - RING + 1)
                if g < NFULL:
                    load_edges(g, r)
                else:
                    sp.dma_start(ea[0:TAILP, r, 0, :], edge_attr[g * STEP:E, :]).then_inc(s_ea[r], 16)

            for i, w in enumerate((W1, W2)):
                sp.dma_start(raw[:, i, :].rearrange("p (k d) -> p k d", k=KD), w.rearrange("(k p) d -> p k d", p=P)
                             ).then_inc(s_w12[i], 16)

            def load_gu(e, k):
                for half, w in enumerate((w_gate, w_up)):
                    sp.dma_start(raw[:, k % SRING, half * H:(half + 1) * H], w[e, k * P:(k + 1) * P, :]
                                 ).then_inc(s_raw[k % SRING], 16)

            def load_dn(e, c):
                r = (GUC + c) % SRING
                kk = KH // DC
                for half in (0, 1):
                    k0 = c * kk + half * kk // 2
                    sp.dma_start(raw[:, r, half * H:(half + 1) * H].rearrange("p (k d) -> p k d", d=D),
                                 w_down[e, k0 * P:(k0 + kk // 2) * P, :].rearrange("(k p) d -> p k d", p=P)
                                 ).then_inc(s_raw[r], 16)

            sp.wait_ge(s_w12l, 2)
            load_gu(0, 1)
            sp.wait_ge(s_ul, NC * KD)
            load_gu(0, 2)
            sp.wait_ge(s_l1, NC * KD)
            load_gu(0, 0)

            def rest(e):
                sp.wait_ge(s_gul, e * GUC + 1)
                load_gu(e, 3)
                for c in range(DC):
                    sp.wait_ge(s_gul, e * GUC + (c + 2))
                    load_dn(e, c)

            rest(0)
            with sp.Fori(1, NX) as e:
                sp.wait_ge(s_gul, e * GUC)
                load_gu(e, 0)
                for k in (1, 2):
                    sp.wait_ge(s_dnl, e * DC - DC + k)
                    load_gu(e, k)
                rest(e)

            sp.wait_ge(s_all, 1)
            most = N // 16 * 16
            sp.dma_start(out[0:most, :].rearrange("(a r) d -> a (r d)", a=16),
                         sum_dram[0:most, :].rearrange("(a r) d -> a (r d)", a=16)).then_inc(s_outd, 16)
            sp.dma_start(out[most:N, :], sum_dram[most:N, :]).then_inc(s_outd, 16)
            sp.wait_ge(s_outd, 32)

        @block.gpsimd
        def _(pool):
            pool.memset(ident[:, :], 0.0).then_inc(s_zero, 1)
            pool.memset(before[:, :], 1.0).then_inc(s_zero, 1)
            pool.memset(ones[:, :], 1.0).then_inc(s_zero, 1)
            pool.memset(y_sb[:, :], 0.0).then_inc(s_zero, 1)
            pool.memset(slot_i[:, :], 0).then_inc(s_zero, 1)
            pool.wait_ge(s_zero, 5)
            pool.affine_select(out=ident[:, :], in_=ident[:, :], compare_op=ALU.not_equal, fill=1.0, base=0,
                               pattern=[[-1, P]], channel_multiplier=1).then_inc(s_const, 1)
            pool.affine_select(out=before[:, :], in_=before[:, :], compare_op=ALU.is_gt, fill=0.0, base=0,
                               pattern=[[1, P]], channel_multiplier=-1).then_inc(s_const, 1)
            pool.iota(node_i[:, :], pattern=[[1, NP]], base=0, channel_multiplier=0).then_inc(s_const, 1)
            pool.iota(tok_i[:, :], pattern=[[P, NT]], base=0, channel_multiplier=1).then_inc(s_const, 1)
            pool.iota(em8_i[:, :], pattern=[[1, NX]], base=-NX, channel_multiplier=0).then_inc(s_const, 1)

            def gathers(g, count, r, parts=P, width=J):
                pool.tensor_copy(idx[:, r, :], srcT[:, bass.ds(g, 1), :].rearrange("p a j -> p (a j)")
                                 ).then_inc(s_idxc, 1)
                pool.wait_ge(s_idxc, count)
                pool.sem_inc(s_idxr, 1)
                for j in range(width):
                    pool.indirect_dma_start(xg[0:parts, r, j, :], None, xn_dram[:, :],
                                            bass.IndirectOffsetOnAxis(ap=idx[0:parts, r, j:j + 1], axis=0)
                                            ).then_inc(s_xg[r], 16)

            pool.wait_ge(s_idx, 1)
            pool.wait_ge(s_xnd, 16 * len(GROUPS))
            for r in range(RING):
                gathers(r, r + 1, r)
            with pool.Fori(1, ROUNDS - 1) as i:
                for r in range(RING):
                    g = i * RING + r
                    pool.wait_ge(s_sum, g - RING + 1)
                    gathers(g, g + 1, r)
            for r in range(RING):
                g = NSTEP - RING + r
                pool.wait_ge(s_sum, g - RING + 1)
                if g < NFULL:
                    gathers(g, g + 1, r)
                else:
                    gathers(g, g + 1, r, TAILP, 1)

            pool.wait_ge(s_sloti, 1)
            pool.wait_ge(s_x2d, 32)

            def rows_of(n):
                pool.indirect_dma_start(rows[:, n % RROWS, :], None, x2_dram[:, :],
                                        bass.IndirectOffsetOnAxis(ap=slot_i[:, n:n + 1], axis=0)
                                        ).then_inc(s_rows, 16)
                pool.wait_ge(s_rows, 16 * (n + 1))
                pool.sem_inc(s_rrdy, 1)

            def add_results(n):
                pool.wait_ge(s_ysb, n + 2)
                pool.wait_ge(s_added, 16 * (n + 1))
                pool.indirect_dma_start(sum_dram[:, :], bass.IndirectOffsetOnAxis(ap=target[:, n:n + 1], axis=0),
                                        y_sb[:, :], None, compute_op=ALU.add).then_inc(s_added, 16)

            for n in range(RROWS):
                rows_of(n)
            pool.dma_start(sum_dram[NP:NP + P, :], y_sb[:, :]).then_inc(s_added, 16)
            pool.wait_ge(s_sum0, 32)
            pool.wait_ge(s_target, 1)
            pool.wait_ge(s_tab, 1)
            for n in range(SLOTS):
                if n < SURE:
                    add_results(n)
                else:
                    with pool.If(flag(pool, 2, n)):
                        add_results(n)
                if n + RROWS <= SLOTS:
                    pool.wait_ge(s_rcur, n + 1)
                    rows_of(n + RROWS)
            last = pool.value_load(last_i[0:1, 0:1], min_val=SURE - 1, max_val=SLOTS - 1)
            pool.wait_ge(s_added, last * 16 + 32)
            pool.sem_inc(s_all, 1)

        @block.scalar
        def _(act):
            act.wait_ge(s_padids, 1)
            for t, v in enumerate((src, dst)):
                act.dma_start(ids_i[0:NFULL, t, :], v[0:NFULL * STEP].rearrange("(g e) -> g e", e=STEP)
                              ).then_inc(s_ids, 16)
                act.dma_start(ids_i[NFULL:NSTEP, t, :].rearrange("g (p j) -> g p j", j=J)[:, 0:TAILP, 0:1],
                              v[NFULL * STEP:E].rearrange("(g e j) -> g e j", g=1, j=1),
                              allow_slow_non_contiguous=True).then_inc(s_ids, 16)
            act.activation(warm[:, 1:2], warm[:, 0:1], ACT.Sqrt)
            for t, v in enumerate((b1, b2, gamma, beta)):
                act.dma_start(vecs[t * KD:(t + 1) * KD, :], v.rearrange("(k p) -> k p", p=P)).then_inc(s_vec, 16)
            act.dma_start(rw[:, :], router_w[:, :]).then_inc(s_vec, 16)
            for g, (a, b) in enumerate(GROUPS):
                act.wait_ge(s_var, g + 1)
                act.activation(rstd[:, a:b], mv[:, a:b, 1], ACT.Sqrt).then_inc(s_std, 1)
                act.wait_ge(s_shift, g + 1)
                act.activation(xn[:, a, :], x_sb[:, a, :], ACT.Identity, bias=shift[:, a:a + 1],
                               scale=rstd[:, a:a + 1]).then_inc(s_xna, 1)
                normed(act, g, b)
                if b < NT:
                    act.dma_start(xrows(xn_dram, a, b), xn[:, a:b, :]).then_inc(s_xnd, 16)
                else:
                    act.dma_start(xn_dram[(NT - 1) * P:N, :], xn[0:LASTN, NT - 1, :]).then_inc(s_xnd, 16)
            act.wait_ge(s_xnd, 16 * len(GROUPS))
            for g, (a, b) in enumerate(GROUPS):
                act.wait_ge(s_agg0, g + 1)
                for c in range(a, b):
                    act.wait_ge(s_xnt, c + 1)
                    act.copy(xnT[:, c, :, :], ps[:, 2 + c % 2, :].rearrange("p (k n) -> p k n", k=KD)
                             ).then_inc(s_xntc, 1)
            def relu(r, count, width=J):
                act.wait_ge(s_sum, count)
                act.activation(ea[:, r, 0:width, :], ea[:, r, 0:width, :], ACT.Relu).then_inc(s_msg, 1)

            with act.Fori(0, ROUNDS - 1) as i:
                for r in range(RING):
                    relu(r, i * RING + (r + 1))
            for r in range(RING):
                g = NSTEP - RING + r
                relu(r, g + 1, J if g < NFULL else 1)

            for i, w in enumerate((W1_h, W2_h)):
                act.wait_ge(s_w12[i], 16)
                act.copy(w[:, :, :], raw[:, i, :].rearrange("p (k d) -> p k d", k=KD)).then_inc(s_w12h, 1)

            def aggregate_high(a, b):
                for c in range(a, b):
                    act.wait_ge(s_tr, c + 1)
                    act.copy(hT_h[:, :, c * P:(c + 1) * P],
                             ps[:, TURNED[c % 4], :].rearrange("p (k n) -> p k n", k=KD)).then_inc(s_trh, 1)

            aggregate_high(0, EARLY)
            for n, (lo, w) in enumerate(CHUNKS):
                for m in range(KD):
                    i = n * KD + m
                    if n == 0 and m < KD - 1:
                        aggregate_high(*LATER[m])
                    if i >= 2:
                        act.wait_ge(s_ul, i - 1)
                    act.wait_ge(s_l1, i + 1)
                    act.activation(u32[:, i % 2, 0:w], ps[:, 5 + i % 2, 0:w], ACT.Relu,
                                   bias=vecT[:, 0, m:m + 1]).then_inc(s_u, 1)
                    act.wait_ge(s_u, i + 1)
                    act.copy(uT_h[:, n % 2, m, 0:w], u32[:, i % 2, 0:w]).then_inc(s_uh, 1)
            def part_gu(k, e):
                act.wait_ge(s_raw[k % SRING], 32 * (e * 2 + (k // SRING + 1)))
                act.copy(gu_h[k][:, :], raw[:, k % SRING, :]).then_inc(s_guh, 1)

            act.wait_ge(s_l1, NC * KD)
            for k in range(SRING):
                part_gu(k, 0)
            act.wait_ge(s_bvar, 1)
            act.activation(bsc[:, 0, :], bmv[:, :, 1], ACT.Sqrt).then_inc(s_bstd, 1)
            act.wait_ge(s_bsc, 1)
            for half in (0, 1):
                cols = slice(half * HALF * P, (half + 1) * HALF * P)
                for m in range(KD // 2):
                    act.activation(oT[:, m, cols], oT[:, m, cols], ACT.Identity, bias=bsc[:, 2, m:m + 1],
                                   scale=bsc[:, 1, m:m + 1]).then_inc(s_bna, 1)
            def token(c):
                act.wait_ge(s_x2t, c + 1)
                act.copy(x2T[:, c % 4, :, :], ps[:, X2_BANKS[c % 3], :].rearrange("p (k n) -> p k n", k=KD)
                         ).then_inc(s_x2ca, 1)

            for half in (0, 1):
                a, b = half * HALF, (half + 1) * HALF
                act.wait_ge(s_var2, half + 1)
                act.activation(rstd[:, a:b], mv[:, a:b, 1], ACT.Sqrt).then_inc(s_std2, 1)
                act.wait_ge(s_shift2, half + 1)
                for c in range(a, b):
                    if c not in X2_DVE:
                        act.activation(xn[:, c, :], x_sb[:, c, :], ACT.Identity, bias=shift[:, c:c + 1],
                                       scale=rstd[:, c:c + 1]).then_inc(s_x2a, 1)
                    if 2 <= c < HALF:
                        token(c - 2)
                act.wait_ge(s_x2a, b - half * len(X2_DVE))
                if half:
                    act.wait_ge(s_x2v, len(X2_DVE))
                act.dma_start(xrows(x2_dram, a, b), xn[:, a:b, :]).then_inc(s_x2d, 16)
                for c in X2T_ACT:
                    if (c >= HALF) if half else (HALF - 2 <= c < HALF):
                        token(c)
                act.dma_start(xrows(sum_dram, a, b), x_sb[:, a:b, :]).then_inc(s_sum0, 16)
            act.wait_ge(s_d, 1)
            act.activation(wt[:, 1, :], wt[:, 0, :], ACT.Exp).then_inc(s_ex, 1)

            def part_dn(c, e):
                r = (GUC + c) % SRING
                act.wait_ge(s_raw[r], 32 * (e * 2 + 2))
                act.copy(dn_h[c][:, :], raw[:, r, :]).then_inc(s_dnh, 1)

            def silu(n):
                act.wait_ge(s_gu, n * GUC + GUC)
                for half in (0, 1):
                    act.activation(hid[:, half * BANK:(half + 1) * BANK], ps[:, half, :], ACT.Silu).then_inc(s_sig, 1)

            def rows_high(n):
                act.wait_ge(s_rt, n + 1)
                act.copy(rT_h[:, :, :], ps[:, 7, :].rearrange("p (k n) -> p k n", k=KD)).then_inc(s_rh, 1)

            def hidden_high(n):
                for half in (0, 1):
                    act.wait_ge(s_ht, n * 2 + (half + 1))
                    act.copy(hidT_h[:, half * 4:half * 4 + 4, :],
                             ps[:, 4 + half, :].rearrange("p (k n) -> p k n", k=4)).then_inc(s_hh, 1)

            act.activation(warm[:, 1:2], warm[:, 0:1], ACT.Silu)
            part_gu(SRING, 0)
            rows_high(0)
            part_dn(0, 0)
            silu(0)
            rows_high(1)
            part_dn(1, 0)
            def next_gate_up(n, pieces):
                e = next_expert(act, n)
                for k in pieces:
                    act.wait_ge(s_gu, n * GUC + (k + 1))
                    part_gu(k, e)

            act.wait_ge(s_tab, 1)
            with act.If(flag(act, 1, 0)):
                next_gate_up(0, range(GUC))
            last = act.value_load(last_i[0:1, 0:1], min_val=SURE - 1, max_val=SLOTS - 1)
            with act.Fori(0, last) as j:
                n = row_tile(j)
                m = n + 1
                hidden_high(n)
                early, ends, late = flag(act, 3, m), flag(act, 1, n), flag(act, 4, m)
                with act.If(early):
                    next_gate_up(m, range(GUC - 1))
                silu(m)
                rows_high(n + 2)
                with act.If(early):
                    next_gate_up(m, [GUC - 1])
                with act.If(ends):
                    e = next_expert(act, n)
                    for c in range(DC):
                        act.wait_ge(s_y, n * DC + (c + 1))
                        part_dn(c, e)
                with act.If(late):
                    next_gate_up(m, range(GUC))
            hidden_high(last)

        @block.vector
        def _(dve):
            chain = [0]

            def fresh(ins):
                chain[0] += 1
                ins.then_inc(s_dve, 1)

            def settled():
                dve.wait_ge(s_dve, chain[0])

            def link(ins):
                fresh(ins)
                settled()

            fresh(dve.memset(warm[:, :], 1.0))
            fresh(dve.memset(ids_i[:, 0, :], 0))
            settled()
            dve.memset(ids_i[:, 1, :], NOWHERE).then_inc(s_padids, 1)
            dve.memset(x_sb[:, NT - 1, :], 0.0).then_inc(s_padx, 1)
            fresh(dve.memset(first[:, :], 0.0))
            fresh(dve.memset(ps[:, 0, :], 0.0))
            settled()
            dve.sem_inc(s_acc, 1)
            dve.sem_inc(s_seg, J)

            def moments(c):
                fresh(dve.bn_stats(stats[:, c, :], x_sb[:, c, :]))

            def variances(a, b):
                settled()
                for c in range(a, b):
                    fresh(dve.bn_aggr(mv[:, c, :], stats[:, c, :]))
                settled()
                return dve.tensor_scalar(mv[:, a:b, 1], mv[:, a:b, 1], EPS, None, ALU.add)

            def shifts(a, b):
                link(dve.reciprocal(rstd[:, a:b], rstd[:, a:b]))
                return dve.scalar_tensor_tensor(out=shift[:, a:b], in0=mv[:, a:b, 0], scalar=-1.0,
                                                in1=rstd[:, a:b], op0=ALU.mult, op1=ALU.mult)

            for g, (a, b) in enumerate(GROUPS):
                dve.wait_ge(s_xin[g], 16)
                for c in range(a, b):
                    moments(c)
                variances(a, b).then_inc(s_var, 1)
                dve.wait_ge(s_std, g + 1)
                shifts(a, b).then_inc(s_shift, 1)
                dve.wait_ge(s_shift, g + 1)
                for c in range(a + 1, b):
                    dve.tensor_scalar(xn[:, c, :], x_sb[:, c, :], rstd[:, c:c + 1], shift[:, c:c + 1],
                                      ALU.mult, ALU.add).then_inc(s_xnv, 1)

            dve.wait_ge(s_ids, 64)
            dve.tensor_copy(ids_f[:, :, :], ids_i[:, :, :]).then_inc(s_idf, 1)
            dve.wait_ge(s_idf, 1)
            dve.tensor_reduce(span[:, 0:1], ids_f[:, 1, :], AX.X, ALU.min).then_inc(s_span, 1)
            dve.tensor_reduce(span[:, 1:2], ids_f[:, 1, :], AX.X, ALU.max).then_inc(s_span, 1)
            dve.wait_ge(s_const, 5)
            fresh(dve.tensor_copy(node[:, :], node_i[:, :]))
            fresh(dve.tensor_copy(tok[:, :], tok_i[:, :]))
            fresh(dve.tensor_copy(em8[:, :], em8_i[:, :]))
            dve.wait_ge(s_tps, 1)
            dve.tensor_copy(srcT[:, :, :], ps[:, 4, 0:J * NSTEP].rearrange("p (j g) -> p g j", j=J)
                            ).then_inc(s_idx, 1)
            fresh(dve.tensor_copy(dstT[:, :, :], ps[:, 5, 0:J * NSTEP].rearrange("p (j g) -> p g j", j=J)))
            dve.wait_ge(s_tps, 2)
            link(dve.tensor_copy(span_i[:, :, :], ps[0:1, 6, 0:2 * NSTEP].rearrange("p (t g) -> p t g", t=2)))
            link(dve.tensor_scalar(span_v[:, :, :], span_i[:, :, :], 7, None, ALU.arith_shift_right))
            link(dve.tensor_copy(span_f[:, :, :], span_v[:, :, :]))
            dve.tensor_scalar(span_v[:, :, :], span_f[:, :, :], float(NT - 1), None, ALU.min).then_inc(s_spanv, 1)
            for g, (a, b) in enumerate(GROUPS):
                normed(dve, g, b)
                dve.tensor_copy(agg[:, a:b, :], xn[:, a:b, :]).then_inc(s_agg0, 1)
            link(dve.tensor_scalar(valid[:, :], tok[:, :], float(N), None, ALU.is_lt))
            fresh(dve.tensor_scalar(nobody[:, :], tok[:, 0:1], float(NP + 1), None, ALU.add))
            fresh(dve.scalar_tensor_tensor(out=tok1[:, :], in0=tok[:, :], scalar=1.0, in1=valid[:, :],
                                           op0=ALU.add, op1=ALU.mult))
            dve.wait_ge(s_tps, 3)
            fresh(dve.tensor_copy(vecT[:, :, :], ps[:, 7, 0:4 * KD].rearrange("p (t k) -> p t k", t=4)))
            fresh(dve.tensor_copy(rwT[:, :, :], ps[:, 7, 4 * KD:4 * KD + KD * NX].rearrange("p (k e) -> p k e", k=KD)))
            settled()

            def add(r, count, width=J):
                dve.wait_ge(s_ea[r], count * 16)
                dve.wait_ge(s_xg[r], count * 16 * J - 16 * (J - width))
                dve.tensor_tensor(ea[:, r, 0:width, :], ea[:, r, 0:width, :], xg[:, r, 0:width, :], ALU.add
                                  ).then_inc(s_sum, 1)

            unit = dve.alloc_register("unit")
            behind = dve.alloc_register("behind")
            dve.reg_mov(unit, 1)
            dve.reg_mov(behind, 0)

            def accumulate(u):
                k = dve.snap(behind, min_val=0, max_val=NT - 1)
                dve.wait_ge(s_seg, u * J)
                dve.wait_ge(s_acc, u)
                a = agg[:, bass.ds(k, 1), :].rearrange("p a d -> p (a d)")
                b = ps[:, bass.ds((u + 1) % 2, 1), :].rearrange("p a d -> p (a d)")
                dve.tensor_tensor(a, a, b, ALU.add).then_inc(s_acc, 1)

            def segment(g, width=J):
                lo, hi = (dve.value_load(span_v[0:1, k, bass.ds(g, 1)], min_val=0, max_val=NT - 1) for k in (0, 1))
                with dve.Fori(lo, hi + 1) as k:
                    u = dve.snap(unit, min_val=1, max_val=NSTEP * NT)
                    for j in range(width):
                        dve.wait_ge(s_seg, u * J - (J - 1) + j)
                        dve.tensor_tensor(onehot[:, j, :], node[:, bass.ds(k * P, P)],
                                          dstT[:, bass.ds(g, 1), j].broadcast_to([P, P]), ALU.is_equal
                                          ).then_inc(s_hot, J // width)
                    accumulate(u)
                    dve.reg_mov(behind, k)
                    dve.reg_add(unit, unit, 1)

            dve.wait_ge(s_agg0, len(GROUPS))
            add(0, 1)
            add(1, 1)
            dve.wait_ge(s_spanv, 1)
            with dve.Fori(0, ROUNDS - 1) as i:
                for r in range(RING):
                    segment(i * RING + r)
                    add((r + 2) % RING, i + 1 + (r + 2) // RING)
            def split_low(i):
                w, h = ((W1_l, W1_h), (W2_l, W2_h))[i]
                dve.wait_ge(s_w12h, i + 1)
                dve.tensor_tensor(w[:, :, :], raw[:, i, :].rearrange("p (k d) -> p k d", k=KD),
                                  h[:, :, :].bitcast(F32), ALU.subtract).then_inc(s_w12l, 1)

            for r in range(RING):
                g = NSTEP - RING + r
                if g == NFULL:
                    split_low(0)
                segment(g, J if g < NFULL else 1)
                if r + 2 < RING:
                    add(r + 2, ROUNDS, J if g + 2 < NFULL else 1)
            accumulate(dve.snap(unit, min_val=1, max_val=NSTEP * NT + 1))
            products = dve.snap(unit, min_val=1, max_val=NSTEP * NT + 1)
            dve.wait_ge(s_acc, products + 1)
            dve.sem_inc(s_agg, 1)

            def aggregate_low(a, b):
                for c in range(a, b):
                    dve.wait_ge(s_trh, c + 1)
                    dve.tensor_tensor(hT_l[:, :, c * P:(c + 1) * P],
                                      ps[:, TURNED[c % 4], :].rearrange("p (k n) -> p k n", k=KD),
                                      hT_h[:, :, c * P:(c + 1) * P].bitcast(F32), ALU.subtract).then_inc(s_trl, 1)

            def hidden_low(n):
                lo, w = CHUNKS[n]
                for m in range(KD):
                    i = n * KD + m
                    if n == 0 and m < KD - 1:
                        aggregate_low(*LATER[m])
                    dve.wait_ge(s_uh, i + 1)
                    dve.tensor_tensor(uT_l[:, n % 2, m, 0:w], u32[:, i % 2, 0:w],
                                      uT_h[:, n % 2, m, 0:w].bitcast(F32), ALU.subtract).then_inc(s_ul, 1)

            def second(n):
                lo, w = CHUNKS[n]
                for m in range(KD):
                    i = n * KD + m
                    dve.wait_ge(s_l2, i + 1)
                    def tiles_of(a):
                        return a.rearrange("p (c n) -> p c n", n=P)
                    dve.scalar_tensor_tensor(out=tiles_of(oT[:, m, lo:lo + w]), in0=tiles_of(ps[:, i % 2, 0:w]),
                                             scalar=vecT[:, 1, m:m + 1], in1=xnT[:, lo // P:(lo + w) // P, m, :],
                                             op0=ALU.add, op1=ALU.add).then_inc(s_l2c, 1)
                    dve.wait_ge(s_l2c, i + 1)
                    fresh(dve.bn_stats(bst[:, m, n, :], oT[:, m, lo:min(lo + w, N)]))

            aggregate_low(0, EARLY)
            hidden_low(0)
            split_low(1)
            for n in range(1, NC):
                hidden_low(n)
                second(n - 1)
            second(NC - 1)
            settled()
            for m in range(KD):
                fresh(dve.bn_aggr(bmv[:, m, :], bst[:, m, :, :].rearrange("p n s -> p (n s)")))
            settled()
            dve.tensor_scalar(bmv[:, :, 1], bmv[:, :, 1], EPS, None, ALU.add).then_inc(s_bvar, 1)
            dve.wait_ge(s_bstd, 1)
            link(dve.reciprocal(bsc[:, 0, :], bsc[:, 0, :]))
            link(dve.tensor_tensor(bsc[:, 1, :], bsc[:, 0, :], vecT[:, 2, :], ALU.mult))
            link(dve.tensor_tensor(bsc[:, 0, :], bmv[:, :, 0], bsc[:, 1, :], ALU.mult))
            dve.tensor_tensor(bsc[:, 2, :], vecT[:, 3, :], bsc[:, 0, :], ALU.subtract).then_inc(s_bsc, 1)
            dve.wait_ge(s_bsc, 1)
            for half in (0, 1):
                cols = slice(half * HALF * P, (half + 1) * HALF * P)
                for m in range(KD // 2, KD):
                    dve.tensor_scalar(oT[:, m, cols], oT[:, m, cols], bsc[:, 1, m:m + 1], bsc[:, 2, m:m + 1],
                                      ALU.mult, ALU.add).then_inc(s_bnd, 1)

            def residual(c):
                dve.wait_ge(s_oTt, c + 1)
                dve.tensor_tensor(x_sb[:, c, :], x_sb[:, c, :], ps[:, X1_BANKS[c % 3], :], ALU.add).then_inc(s_x1, 1)

            def x1_moments(c):
                dve.wait_ge(s_x1, c + 1)
                moments(c)

            def token(c):
                dve.wait_ge(s_x2t, c + 1)
                dve.tensor_copy(x2T[:, c % 4, :, :], ps[:, X2_BANKS[c % 3], :].rearrange("p (k n) -> p k n", k=KD)
                                ).then_inc(s_x2cv, 1)

            residual(0)
            for half in (0, 1):
                a, b = half * HALF, (half + 1) * HALF
                for c in range(a, b):
                    if c + 1 < NT:
                        residual(c + 1)
                    x1_moments(c)
                variances(a, b).then_inc(s_var2, 1)
                if half:
                    token(X2T_DVE[0])
                dve.wait_ge(s_std2, half + 1)
                shifts(a, b).then_inc(s_shift2, 1)
            dve.wait_ge(s_shift2, 2)
            for c in X2_DVE:
                dve.tensor_scalar(xn[:, c, :], x_sb[:, c, :], rstd[:, c:c + 1], shift[:, c:c + 1],
                                  ALU.mult, ALU.add).then_inc(s_x2v, 1)
            for c in X2T_DVE[1:]:
                token(c)

            def part_gu(k, e):
                dve.wait_ge(s_guh, e * GUC + (k + 1))
                dve.tensor_tensor(gu_l[k][:, :], raw[:, k % SRING, :], gu_h[k][:, :].bitcast(F32),
                                  ALU.subtract).then_inc(s_gul, 1)

            part_gu(0, 0)

            def spread(v):
                return v.unsqueeze(2).broadcast_to([P, NT, NX])

            em8_b = em8[:, :].unsqueeze(1).broadcast_to([P, NT, NX])
            dve.wait_ge(s_log, NT)
            link(dve.tensor_copy(L[:, :, :], ps[:, 2, 0:NT * NX].rearrange("p (c e) -> p c e", e=NX)))
            for k, (logit, mask) in enumerate(((L, M1), (L2, M2))):
                link(dve.tensor_reduce(v12[:, k, :], logit[:, :, :], AX.X, ALU.max))
                link(dve.tensor_tensor(t8[:, :, :], logit[:, :, :], spread(v12[:, k, :]), ALU.is_equal))
                link(dve.tensor_tensor(t8[:, :, :], t8[:, :, :], em8_b, ALU.mult))
                link(dve.tensor_reduce(i12[:, k, :], t8[:, :, :], AX.X, ALU.min))
                link(dve.tensor_tensor(mask[:, :, :], em8_b, spread(i12[:, k, :]), ALU.is_equal))
                if k == 0:
                    link(dve.scalar_tensor_tensor(out=L2[:, :, :], in0=M1[:, :, :], scalar=FAR, in1=L[:, :, :],
                                                  op0=ALU.mult, op1=ALU.add))
            dve.tensor_tensor(wt[:, 0, :], v12[:, 1, :], v12[:, 0, :], ALU.subtract).then_inc(s_d, 1)
            fresh(dve.tensor_tensor(M1[:, :, :], M1[:, :, :], spread(valid[:, :]), ALU.mult))
            fresh(dve.tensor_tensor(M2[:, :, :], M2[:, :, :], spread(valid[:, :]), ALU.mult))
            settled()
            dve.tensor_tensor(M[:, :, :], M1[:, :, :], M2[:, :, :], ALU.add).then_inc(s_M, 1)

            upto = L[:, 0:NX, :]
            fresh(dve.tensor_tensor(upto, em8[:, :].unsqueeze(1).broadcast_to([P, NX, NX]),
                                    em8[:, :].unsqueeze(2).broadcast_to([P, NX, NX]), ALU.is_le))
            dve.wait_ge(s_rank, 1)
            link(dve.tensor_reduce(cnt[:, :], ps[:, 1, 0:NT * NX].rearrange("p (c e) -> p e c", e=NX), AX.X, ALU.add))
            link(dve.tensor_scalar(cnt_i[:, 0, :], cnt[:, :], float(P - 1), None, ALU.add))
            link(dve.tensor_scalar(cnt_i[:, 1, :], cnt_i[:, 0, :], 7, None, ALU.arith_shift_right))
            link(dve.tensor_scalar(tiles[:, :], cnt_i[:, 1, :], 1.0, None, ALU.max))
            link(dve.tensor_tensor(t8[:, 0:NX, :], upto, tiles[:, :].unsqueeze(1).broadcast_to([P, NX, NX]), ALU.mult))
            link(dve.tensor_reduce(first[:, 1:NX + 1], t8[:, 0:NX, :], AX.X, ALU.add))
            link(dve.scalar_tensor_tensor(out=t8[:, :, :],
                                          in0=first[:, 0:NX].unsqueeze(1).broadcast_to([P, NT, NX]), scalar=float(P),
                                          in1=ps[:, 0, 0:NT * NX].rearrange("p (c e) -> p c e", e=NX),
                                          op0=ALU.mult, op1=ALU.add))
            fresh(dve.tensor_tensor(t9[:, :, :], t8[:, :, :], M1[:, :, :], ALU.mult))
            fresh(dve.tensor_tensor(L2[:, :, :], t8[:, :, :], M2[:, :, :], ALU.mult))
            settled()
            fresh(dve.tensor_reduce(pos[:, 0, :], t9[:, :, :], AX.X, ALU.add))
            fresh(dve.tensor_reduce(pos[:, 1, :], L2[:, :, :], AX.X, ALU.add))
            settled()
            link(dve.tensor_copy(pos_i[:, :, :], pos[:, :, :]))
            flat = pos_i[:, :, :].rearrange("p k c -> p (k c)")
            fresh(dve.tensor_scalar(ps_i[:, 0, :], flat, P - 1, None, ALU.bitwise_and))
            fresh(dve.tensor_scalar(ps_i[:, 1, :], flat, 7, None, ALU.arith_shift_right))
            settled()
            link(dve.tensor_copy(ps_f[:, :, :], ps_i[:, :, :]))
            link(dve.tensor_tensor(slotE[:, :, :], node[:, 0:SLOTS].unsqueeze(1).broadcast_to([P, 2 * NT, SLOTS]),
                                   ps_f[:, 1, :].unsqueeze(2).broadcast_to([P, 2 * NT, SLOTS]), ALU.is_equal))
            for k in (0, 1):
                part = slice(k * NT, (k + 1) * NT)
                fresh(dve.tensor_tensor(slotB[:, part, :], slotE[:, part, :],
                                        tok1[:, :].unsqueeze(2).broadcast_to([P, NT, SLOTS]), ALU.mult))
            settled()
            for t in range(2 * NT):
                dve.tensor_scalar(hot[:, t, :], node[:, 0:P], ps_f[:, 0, t:t + 1], None, ALU.is_equal
                                  ).then_inc(s_hotr, 1)
            dve.wait_ge(s_slot, 1)
            dve.tensor_scalar(slot_i[:, 0:SLOTS], ps[:, 2, 0:SLOTS], -1.0, 0.0, ALU.add, ALU.max).then_inc(s_sloti, 1)
            link(dve.tensor_scalar(unused[:, :], ps[:, 2, 0:SLOTS], 0.0, nobody[:, :], ALU.is_equal, ALU.mult))
            dve.scalar_tensor_tensor(out=target[:, :], in0=ps[:, 2, 0:SLOTS], scalar=-1.0, in1=unused[:, :],
                                     op0=ALU.add, op1=ALU.add).then_inc(s_target, 1)
            part_gu(1, 0)
            def part_dn(c, e):
                dve.wait_ge(s_dnh, e * DC + (c + 1))
                dve.tensor_tensor(dn_l[c][:, :], raw[:, (GUC + c) % SRING, :], dn_h[c][:, :].bitcast(F32),
                                  ALU.subtract).then_inc(s_dnl, 1)

            def row_copy(n):
                if not isinstance(n, int) or n:
                    dve.wait_ge(s_rt, n)
                dve.wait_ge(s_rrdy, n + 1)
                dve.tensor_scalar(row_cur[:, :], rows[:, bass.ds(n % RROWS, 1), :].rearrange("p a d -> p (a d)"),
                                  1.0, None, ALU.mult).then_inc(s_rcur, 1)

            def rows_low(n):
                dve.wait_ge(s_rh, n + 1)
                dve.tensor_tensor(rT_l[:, :, :], ps[:, 7, :].rearrange("p (k n) -> p k n", k=KD),
                                  rT_h[:, :, :].bitcast(F32), ALU.subtract).then_inc(s_rl, 1)

            def multiply(n):
                for half in (0, 1):
                    dve.wait_ge(s_sig, n * 2 + (half + 1))
                    a = slice(half * BANK, (half + 1) * BANK)
                    dve.tensor_tensor(hid[:, a], hid[:, a], ps[:, 2 + half, :], ALU.mult).then_inc(s_hid, 1)

            def hidden_low_part(n):
                for half in (0, 1):
                    dve.wait_ge(s_hh, n * 2 + (half + 1))
                    a = slice(half * 4, half * 4 + 4)
                    dve.tensor_tensor(hidT_l[:, a, :], ps[:, 4 + half, :].rearrange("p (k n) -> p k n", k=4),
                                      hidT_h[:, a, :].bitcast(F32), ALU.subtract).then_inc(s_hl, 1)

            def result(n):
                dve.wait_ge(s_added, n * 16 + 16)
                dve.wait_ge(s_y, n * DC + DC)
                dve.tensor_scalar(y_sb[:, :], ps[:, 6, :], w_slot[:, bass.ds(n, 1)], None, ALU.mult
                                  ).then_inc(s_ysb, 1)

            row_copy(0)
            dve.wait_ge(s_ex, 1)
            link(dve.tensor_scalar(wt[:, 2, :], wt[:, 1, :], 1.0, None, ALU.add))
            link(dve.reciprocal(w12[:, 0, :], wt[:, 2, :]))
            link(dve.tensor_tensor(w12[:, 1, :], wt[:, 1, :], w12[:, 0, :], ALU.mult))
            link(dve.tensor_tensor(w12[:, :, :], w12[:, :, :], valid[:, :].unsqueeze(1).broadcast_to([P, 2, NT]),
                                   ALU.mult))
            w_all = w12[:, :, :].rearrange("p k c -> p (k c)")
            link(dve.tensor_copy(w_part[:, 0, :], w_all))
            link(dve.tensor_tensor(w_rest[:, 0, :], w_all, w_part[:, 0, :], ALU.subtract))
            link(dve.tensor_scalar(w_part[:, 1, :], w_rest[:, 0, :], 2048.0, None, ALU.mult))
            link(dve.scalar_tensor_tensor(out=w_rest[:, 1, :], in0=w_rest[:, 0, :], scalar=2048.0,
                                          in1=w_part[:, 1, :], op0=ALU.mult, op1=ALU.subtract))
            link(dve.tensor_scalar(w_part[:, 2, :], w_rest[:, 1, :], 2048.0, None, ALU.mult))

            rows_low(0)
            part_gu(2, 0)
            part_gu(3, 0)
            row_copy(1)
            for i in range(3):
                dve.tensor_tensor(slotW[:, :, i, :], slotE[:, :, :],
                                  w_part[:, i, :].unsqueeze(2).broadcast_to([P, 2 * NT, SLOTS]), ALU.mult
                                  ).then_inc(s_wparts, 1)
            starts = first[0:1, 1:NX].unsqueeze(1).broadcast_to([1, SLOTS, NX - 1])
            fresh(dve.tensor_tensor(cmp7[:, 0, :, :], node[0:1, 0:SLOTS].unsqueeze(2).broadcast_to([1, SLOTS, NX - 1]),
                                    starts, ALU.is_ge))
            fresh(dve.tensor_tensor(cmp7[:, 1, :, :],
                                    node[0:1, 1:SLOTS + 1].unsqueeze(2).broadcast_to([1, SLOTS, NX - 1]),
                                    starts, ALU.is_equal))
            settled()
            fresh(dve.tensor_reduce(tile_f[:, 0:2, :], cmp7[:, :, :, :], AX.X, ALU.add))
            fresh(dve.tensor_scalar(tile_f[:, 2, :], node[0:1, 0:SLOTS], first[0:1, NX:NX + 1], None, ALU.is_lt))
            fresh(dve.memset(tile_f[:, 4, 0:1], 0.0))
            settled()
            fresh(dve.tensor_tensor(tile_f[:, 4, 1:SLOTS], tile_f[:, 1, 1:SLOTS], tile_f[:, 1, 0:SLOTS - 1], ALU.mult))
            settled()
            link(dve.tensor_tensor(tile_f[:, 3, :], tile_f[:, 1, :], tile_f[:, 4, :], ALU.subtract))
            fresh(dve.tensor_copy(tile_v[:, :, :], tile_f[:, :, :]))
            fresh(dve.tensor_scalar(last_i[:, :], first[0:1, NX:NX + 1], -1.0, None, ALU.add))
            settled()
            dve.sem_inc(s_tab, 1)

            multiply(0)
            rows_low(1)
            dve.wait_ge(s_wslot, 1)
            link(dve.tensor_copy(w_slot[:, :], ps[:, 6, 2 * SLOTS:3 * SLOTS]))
            for i in (1, 0):
                link(dve.scalar_tensor_tensor(out=w_sum[:, :] if i else w_slot[:, :],
                                              in0=w_slot[:, :] if i else w_sum[:, :], scalar=1.0 / 2048,
                                              in1=ps[:, 6, i * SLOTS:(i + 1) * SLOTS], op0=ALU.mult, op1=ALU.add))
            dve.sem_inc(s_ysb, 1)
            for c in range(DC):
                part_dn(c, 0)
            def next_gate_up(n, pieces):
                e = next_expert(dve, n)
                for k in pieces:
                    part_gu(k, e)

            with dve.If(flag(dve, 1, 0)):
                next_gate_up(0, range(GUC))
            last = dve.value_load(last_i[0:1, 0:1], min_val=SURE - 1, max_val=SLOTS - 1)
            with dve.Fori(0, last) as j:
                n = row_tile(j)
                m = n + 1
                hidden_low_part(n)
                row_copy(n + 2)
                early, ends, late = flag(dve, 3, m), flag(dve, 1, n), flag(dve, 4, m)
                with dve.If(early):
                    next_gate_up(m, range(GUC - 1))
                multiply(m)
                rows_low(n + 2)
                with dve.If(early):
                    next_gate_up(m, [GUC - 1])
                result(n)
                with dve.If(ends):
                    e = next_expert(dve, n)
                    for c in range(DC):
                        part_dn(c, e)
                with dve.If(late):
                    next_gate_up(m, range(GUC))
            hidden_low_part(last)
            result(last)

        @block.tensor
        def _(pe):
            def turn(bank, c0, source, parts=P):
                cols = source.shape[-1]
                return pe.transpose(ps[0:cols, bank, c0:c0 + parts], source, ident[0:parts, 0:parts])

            def three(outs, left, right, first, last):
                lh, ll = left
                for o, (rh, rl) in zip(outs, right):
                    pe.matmul(o, lh, rh, start=first, stop=False, skip_group_check=True)
                for o, (rh, rl) in zip(outs, right):
                    pe.matmul(o, lh, rl, start=False, stop=False, skip_group_check=True)
                for o, (rh, rl) in zip(outs, right):
                    ins = pe.matmul(o, ll, rh, start=False, stop=last, skip_group_check=True)
                return ins

            pe.wait_ge(s_const, 2)
            pe.wait_ge(s_idf, 1)
            for t, bank in ((0, 4), (1, 5)):
                for j in range(J):
                    last = turn(bank, j * NSTEP, ids_f[:, t, :].rearrange("g (p j) -> g j p", j=J)[:, j, :], NSTEP)
            last.then_inc(s_tps, 1)
            pe.wait_ge(s_span, 2)
            for t in (0, 1):
                last = turn(6, t * NSTEP, span[:, t:t + 1], NSTEP)
            last.then_inc(s_tps, 1)
            pe.wait_ge(s_vec, 80)
            turn(7, 0, vecs[:, :], 4 * KD)
            for k in range(KD):
                last = turn(7, 4 * KD + k * NX, rw[:, k * P:(k + 1) * P], NX)
            last.then_inc(s_tps, 1)

            for g, (a, b) in enumerate(GROUPS):
                normed(pe, g, b)
                for c in range(a, b):
                    if c >= 2:
                        pe.wait_ge(s_xntc, c - 1)
                    for k in range(KD):
                        last = turn(2 + c % 2, k * P, xn[:, c, k * P:(k + 1) * P])
                    last.then_inc(s_xnt, 1)
            pe.wait_ge(s_xntc, NT)

            unit = pe.alloc_register("unit")
            pe.reg_mov(unit, 1)

            def segment(g, r, count, width=J):
                lo, hi = (pe.value_load(span_v[0:1, k, bass.ds(g, 1)], min_val=0, max_val=NT - 1) for k in (0, 1))
                with pe.Fori(lo, hi + 1) as k:
                    u = pe.snap(unit, min_val=1, max_val=NSTEP * NT)
                    pe.wait_ge(s_msg, count)
                    pe.wait_ge(s_acc, u)
                    acc = ps[:, bass.ds(u % 2, 1), :].rearrange("p a d -> p (a d)")
                    parts = P if width == J else TAILP
                    for j in range(width):
                        pe.wait_ge(s_hot, u * J - (J - 1) + j)
                        pe.matmul(acc, onehot[0:parts, j, :], ea[0:parts, r, j, :], start=(j == 0),
                                  stop=(j == width - 1)).then_inc(s_seg, J // width)
                    pe.reg_add(unit, unit, 1)
                pe.matmul(ps[:, 2, 0:1], ident[:, :], ident[:, 0:1], start=True, stop=True).then_inc(s_step, 1)

            pe.wait_ge(s_spanv, 1)
            with pe.Fori(0, ROUNDS - 1) as i:
                for r in range(RING):
                    segment(i * RING + r, r, i * RING + (r + 1))
            for r in range(RING):
                g = NSTEP - RING + r
                segment(g, r, g + 1, J if g < NFULL else 1)

            def turn_aggregate(a, b):
                for c in range(a, b):
                    if c >= 4:
                        pe.wait_ge(s_trl, c - 3)
                    for k in range(KD):
                        last = turn(TURNED[c % 4], k * P, agg[:, c, k * P:(k + 1) * P])
                    last.then_inc(s_tr, 1)

            pe.wait_ge(s_agg, 1)
            turn_aggregate(0, EARLY)
            pe.wait_ge(s_w12l, 1)

            def first_layer(n):
                lo, w = CHUNKS[n]
                pe.wait_ge(s_trl, (lo + w) // P)
                for m in range(KD):
                    i = n * KD + m
                    if i >= 2:
                        pe.wait_ge(s_u, i - 1)
                    for k in range(KD):
                        cols = slice(m * P, (m + 1) * P)
                        last = three([ps[:, 5 + i % 2, 0:w]], (W1_h[:, k, cols], W1_l[:, k, cols]),
                                     [(hT_h[:, k, lo:lo + w], hT_l[:, k, lo:lo + w])], k == 0, k == KD - 1)
                    last.then_inc(s_l1, 1)
                    if n == 0 and m < KD - 1:
                        turn_aggregate(*LATER[m])

            def second_layer(n):
                lo, w = CHUNKS[n]
                pe.wait_ge(s_ul, (n + 1) * KD)
                for m in range(KD):
                    i = n * KD + m
                    if i >= 2:
                        pe.wait_ge(s_l2c, i - 1)
                    cols = slice(m * P, (m + 1) * P)
                    for k in range(KD):
                        last = three([ps[:, i % 2, 0:w]], (W2_h[:, k, cols], W2_l[:, k, cols]),
                                     [(uT_h[:, n % 2, k, 0:w], uT_l[:, n % 2, k, 0:w])], k == 0, k == KD - 1)
                    last.then_inc(s_l2, 1)

            first_layer(0)
            for n in range(1, NC):
                first_layer(n)
                if n == 1:
                    pe.wait_ge(s_w12l, 2)
                second_layer(n - 1)
            second_layer(NC - 1)

            def keep_warm(n, bank=6):
                for _ in range(n):
                    pe.matmul(ps[:, bank, :], ones[:, :], node[:, 0:BANK], start=True, stop=True)

            keep_warm(18)

            def turn_layer(c):
                if c % HALF == 0:
                    pe.wait_ge(s_bna, (c // HALF + 1) * KD // 2)
                    pe.wait_ge(s_bnd, (c // HALF + 1) * KD // 2)
                if c >= 3:
                    pe.wait_ge(s_x1, c - 2)
                for m in range(KD):
                    last = turn(X1_BANKS[c % 3], m * P, oT[:, m, c * P:(c + 1) * P])
                last.then_inc(s_oTt, 1)

            def turn_token(c):
                if c in X2_DVE:
                    pe.wait_ge(s_x2v, c - X2_DVE[0] + 1)
                else:
                    pe.wait_ge(s_x2a, c + 1 if c < HALF else c + 1 - len(X2_DVE))
                for k in range(KD):
                    last = turn(X2_BANKS[c % 3], k * P, xn[:, c, k * P:(k + 1) * P])
                last.then_inc(s_x2t, 1)

            def logits(c):
                if c in X2T_ACT:
                    pe.wait_ge(s_x2ca, X2T_ACT.index(c) + 1)
                else:
                    pe.wait_ge(s_x2cv, X2T_DVE.index(c) + 1)
                for k in range(KD):
                    last = pe.matmul(ps[:, 2, c * NX:(c + 1) * NX], x2T[:, c % 4, k, :], rwT[:, k, :],
                                     start=(k == 0), stop=(k == KD - 1))
                last.then_inc(s_log, 1)

            LEAD = 2
            for c in range(NT):
                if c >= 3:
                    keep_warm(10 if c == HALF else 3)
                turn_layer(c)
                if c >= NT - LEAD:
                    turn_token(c - (NT - LEAD))
            for c in range(NT):
                if c + LEAD < NT:
                    turn_token(c + LEAD)
                if c < NT - 1:
                    keep_warm(1)
                logits(c)
            pe.wait_ge(s_M, 1)
            Mf = M[:, :, :].rearrange("p c e -> p (c e)")
            pe.matmul(ps[:, 0, 0:NT * NX], before[:, :], Mf, start=True, stop=False, skip_group_check=True)
            for d in range(1, NT):
                pe.matmul(ps[:, 0, d * NX:NT * NX], ones[:, :], Mf[:, 0:(NT - d) * NX],
                          start=False, stop=(d == NT - 1), skip_group_check=True)
            last = pe.matmul(ps[:, 1, 0:NT * NX], ones[:, :], Mf, start=True, stop=True)
            last.then_inc(s_rank, 1)
            for t in range(2 * NT):
                pe.wait_ge(s_hotr, t + 1)
                last = pe.matmul(ps[:, 2, 0:SLOTS], hot[:, t, :], slotB[:, t, :], start=(t == 0), stop=(t == 2 * NT - 1))
            last.then_inc(s_slot, 1)
            keep_warm(8)

            def turn_rows(n):
                pe.wait_ge(s_rcur, n + 1)
                for k in range(KD):
                    last = turn(7, k * P, row_cur[:, k * P:(k + 1) * P])
                last.then_inc(s_rt, 1)

            def gate_up(n, e):
                pe.wait_ge(s_rl, n + 1)
                for k in range(KD):
                    pe.wait_ge(s_gul, e * GUC + (k + 1))
                    halves = [slice(b * BANK, (b + 1) * BANK) for b in range(PIECE // BANK)]
                    three([ps[:, b, :] for b in range(PIECE // BANK)], (rT_h[:, k, :], rT_l[:, k, :]),
                          [(gu_h[k][:, a], gu_l[k][:, a]) for a in halves], k == 0, k == KD - 1).then_inc(s_gu, 1)

            def turn_hidden(n):
                for half in (0, 1):
                    pe.wait_ge(s_hid, n * 2 + (half + 1))
                    for k in range(4):
                        a = (half * 4 + k) * P
                        last = turn(4 + half, k * P, hid[:, a:a + P])
                    last.then_inc(s_ht, 1)

            def down(n, e):
                pe.wait_ge(s_ysb, n + 1)
                kk = KH // DC
                for c in range(DC):
                    pe.wait_ge(s_dnl, e * DC + (c + 1))
                    pe.wait_ge(s_hl, n * 2 + (c + 1))
                    for i in range(kk):
                        k = c * kk + i
                        a = slice(i * D, (i + 1) * D)
                        last = three([ps[:, 6, :]], (hidT_h[:, k, :], hidT_l[:, k, :]),
                                     [(dn_h[c][:, a], dn_l[c][:, a])], k == 0, k == KH - 1)
                    last.then_inc(s_y, 1)

            def expert_of(n):
                return pe.value_load(tile_v[0:1, 0, bass.ds(n, 1)], min_val=0, max_val=NX - 1)

            turn_rows(0)
            keep_warm(3)
            gate_up(0, 0)
            pe.wait_ge(s_wparts, 3)
            for t in range(2 * NT):
                last = pe.matmul(ps[:, 6, 0:3 * SLOTS], hot[:, t, :],
                                 slotW[:, t, :, :].rearrange("p i n -> p (i n)"), start=(t == 0), stop=(t == 2 * NT - 1))
            last.then_inc(s_wslot, 1)
            turn_rows(1)
            pe.wait_ge(s_tab, 1)
            last = pe.value_load(last_i[0:1, 0:1], min_val=SURE - 1, max_val=SLOTS - 1)
            with pe.Fori(0, last) as j:
                n = row_tile(j)
                turn_hidden(n)
                gate_up(n + 1, expert_of(n + 1))
                turn_rows(n + 2)
                down(n, expert_of(n))
            turn_hidden(last)
            keep_warm(8, 0)
            down(last, NX - 1)


_INS = ['x', 'src', 'dst', 'edge_attr_512', 'L0_gnn_W1', 'L0_gnn_b1', 'L0_gnn_W2', 'L0_gnn_b2', 'L0_gnn_gamma',
        'L0_gnn_beta', 'L0_ffn_router_w', 'L0_ffn_w_gate', 'L0_ffn_w_up', 'L0_ffn_w_down']


def kernel(**inputs):
    import numpy as _np
    import concourse.bacc as _bacc
    from concourse import mybir as _mybir
    from concourse.bass_utils import run_bass_kernel_spmd as _run

    nc = _bacc.Bacc("TRN2", target_bir_lowering=False, num_devices=1)
    arrays, args = {}, []
    for name in _INS:
        a = _np.ascontiguousarray(inputs[name])
        arrays[f"in_{name}_dram"] = a
        args.append(nc.dram_tensor(f"in_{name}_dram", a.shape, _mybir.dt.from_np(a.dtype), kind="ExternalInput").ap())
    out = nc.dram_tensor("out_0_dram", inputs["x"].shape, _mybir.dt.from_np(_np.dtype("float32")),
                         kind="ExternalOutput").ap()
    gnn_moe_program(nc, *args, out)
    r = _run(nc, [arrays], core_ids=[0])
    return r.results[0]["out_0_dram"]
```
